# Optimizing a Trainium2 kernel written in Bass

```python
import numpy as np
import jax
import jax.numpy as jnp

def _softmax(x, axis=-1):
    return jax.nn.softmax(x, axis=axis)

def _gelu(x):
    return jax.nn.gelu(x, approximate=True)

def _silu(x):
    return jax.nn.silu(x)

def _sigmoid(x):
    return jax.nn.sigmoid(x)

def _layernorm(x, axis=-1, eps=1e-05):
    m = jnp.mean(x, axis=axis, keepdims=True)
    v = jnp.var(x, axis=axis, keepdims=True)
    return (x - m) / jnp.sqrt(v + eps)

def _scatter_add(tgt, idx, src, axis=0):
    return tgt.at[idx].add(src)

def _segment_sum(src, seg, n):
    return jax.ops.segment_sum(src, seg, n)
kernel_name = 'mk_flamingo_gated_d1_seqx_r4_42fcfd'

def setup_inputs(seed: int=0):
    np.random.seed(seed)
    _w = jnp.asarray

    def _rec_inputs():
        import jax
        import jax.numpy as jnp
        _rk = jax.random.key(seed)
        x = 7.22e-05 + 1 * jax.random.normal(jax.random.fold_in(_rk, 1), (8, 256, 256), jnp.float32)
        _lenS = 256 - jax.random.randint(jax.random.fold_in(_rk, 7), (8,), 0, max(1, 256 // 4) + 1, jnp.int32)
        _lenS2 = 256 - jax.random.randint(jax.random.fold_in(_rk, 8), (8,), 0, max(1, 256 // 4) + 1, jnp.int32)
        _ctx_1024P = jax.random.normal(jax.random.fold_in(_rk, 11), (8, 16, 256), jnp.float32)
        _ctx_1024c = jax.random.dirichlet(jax.random.fold_in(_rk, 511), 0.3 * jnp.ones((16,), jnp.float32), (8, 256))
        _ctx_1024t = jnp.einsum('bsk,bkd->bsd', _ctx_1024c, _ctx_1024P)
        _ctx_1024t = _ctx_1024t * jax.lax.rsqrt(jnp.mean(jnp.square(_ctx_1024t)) + 1e-12) * 0.953939
        ctx_1024 = 4.13588e-05 + 0.999923 * (_ctx_1024t + 0.3 * jax.random.normal(jax.random.fold_in(_rk, 611), (8, 256, 256), jnp.float32))
        _g = jax.random.normal(jax.random.fold_in(_rk, 9001), (2, 1), jnp.float32)
        _g = jnp.sign(_g) * jnp.maximum(jnp.abs(_g), 1.0) + (_g == 0) * 1.0
        g_xattn = _g[0]
        g_ffn = _g[1]
        return (x, ctx_1024, g_xattn, g_ffn)
    x, ctx_1024, g_xattn, g_ffn = _rec_inputs()

    def _L0_xattn_setup():
        import jax, jax.numpy as jnp
        import numpy as np
        THETA = 10000.0
        SCALE_BASE = 512.0
        GAMMA = 0.96875

        def _dup_interleave(x):
            return jnp.repeat(x, 2, axis=-1)

        def _xpos(x, offset, inverse_scale):
            L, d = (x.shape[-2], x.shape[-1])
            half = d // 2
            base = (jnp.arange(0, d, 2, dtype=x.dtype) + 0.4 * d) / (1.4 * d)
            pos = jnp.arange(offset, offset + L, dtype=x.dtype)
            scale = base[None, :] ** (pos[:, None] / SCALE_BASE)
            freqs = 1.0 / THETA ** (jnp.arange(half, dtype=x.dtype) / half)
            sin_in = pos[:, None] * freqs[None, :]
            if inverse_scale:
                scale = 1.0 / scale
            sin = _dup_interleave(jnp.sin(sin_in) * scale)
            cos = _dup_interleave(jnp.cos(sin_in) * scale)
            rot = jnp.stack((-x[..., 1::2], x[..., ::2]), axis=-1).reshape(x.shape)
            return x * cos + rot * sin

        def _decay_mask(L, gamma, dtype):
            u = jnp.arange(L, dtype=dtype)[:, None]
            v = jnp.arange(L, dtype=dtype)[None, :]
            return jnp.where(u >= v, gamma ** (u - v), jnp.zeros((), dtype))
        key = jax.random.key(seed)
        ks = jax.random.split(key, 6)
        B, L, E = (2, 1024, 256)
        query = jax.random.normal(ks[0], (B, L, E), jnp.float32)
        k_in = jax.random.normal(ks[1], (B, L, E), jnp.float32)
        value = jax.random.normal(ks[2], (B, L, E), jnp.float32)
        s = 1.0 / np.sqrt(E)
        Wq = jax.random.normal(ks[3], (E, E), jnp.float32) * s
        Wk = jax.random.normal(ks[4], (E, E), jnp.float32) * s
        Wv = jax.random.normal(ks[5], (E, E), jnp.float32) * s
        return {'query': query, 'key': k_in, 'value': value, 'Wq': Wq, 'Wk': Wk, 'Wv': Wv}
    _L0_xattn_all = _L0_xattn_setup()
    _L0_xattn_in = {k: v for k, v in _L0_xattn_all.items() if k in ('Wq', 'Wk', 'Wv')}
    del _L0_xattn_all

    def _L0_ffn_setup():
        import jax, jax.numpy as jnp
        import numpy as np
        DIM = 256
        HID = 512
        E = 8
        K = 2
        R = 16
        B_, S_ = (2, 256)

        def _lora_in(xf, W, b, A, B):
            base = jnp.einsum('td,ehd->teh', xf, W)
            low = jnp.einsum('ter,ehr->teh', jnp.einsum('td,erd->ter', xf, A), B)
            return base + low + b

        def _lora_out(g, W, b, A, B):
            base = jnp.einsum('teh,edh->ted', g, W)
            low = jnp.einsum('ter,edr->ted', jnp.einsum('teh,erh->ter', g, A), B)
            return base + low + b
        key = jax.random.key(seed)
        ks = jax.random.split(key, 14)
        n = lambda k, shape, scale: jax.random.normal(k, shape, jnp.float32) * scale
        inp = {'x': jax.random.normal(ks[0], (B_, S_, DIM), jnp.float32), 'Wg': n(ks[1], (E, DIM), DIM ** (-0.5)), 'W1': n(ks[2], (E, HID, DIM), DIM ** (-0.5)), 'b1': jnp.zeros((E, HID), jnp.float32), 'A1': n(ks[3], (E, R, DIM), DIM ** (-0.5)), 'B1': n(ks[4], (E, HID, R), 0.01), 'W2': n(ks[5], (E, DIM, HID), HID ** (-0.5)), 'b2': jnp.zeros((E, DIM), jnp.float32), 'A2': n(ks[6], (E, R, HID), HID ** (-0.5)), 'B2': n(ks[7], (E, DIM, R), 0.01), 'W3': n(ks[8], (E, HID, DIM), DIM ** (-0.5)), 'b3': jnp.zeros((E, HID), jnp.float32), 'A3': n(ks[9], (E, R, DIM), DIM ** (-0.5)), 'B3': n(ks[10], (E, HID, R), 0.01)}
        return inp
    _L0_ffn_all = _L0_ffn_setup()
    _L0_ffn_in = {k: v for k, v in _L0_ffn_all.items() if k in ('Wg', 'W1', 'b1', 'A1', 'B1', 'W2', 'b2', 'A2', 'B2', 'W3', 'b3', 'A3', 'B3')}
    del _L0_ffn_all
    return {'x': x, 'ctx_1024': ctx_1024, 'g_xattn': g_xattn, 'g_ffn': g_ffn, 'L0_xattn_Wq': _L0_xattn_in['Wq'], 'L0_xattn_Wk': _L0_xattn_in['Wk'], 'L0_xattn_Wv': _L0_xattn_in['Wv'], 'L0_ffn_Wg': _L0_ffn_in['Wg'], 'L0_ffn_W1': _L0_ffn_in['W1'], 'L0_ffn_b1': _L0_ffn_in['b1'], 'L0_ffn_A1': _L0_ffn_in['A1'], 'L0_ffn_B1': _L0_ffn_in['B1'], 'L0_ffn_W2': _L0_ffn_in['W2'], 'L0_ffn_b2': _L0_ffn_in['b2'], 'L0_ffn_A2': _L0_ffn_in['A2'], 'L0_ffn_B2': _L0_ffn_in['B2'], 'L0_ffn_W3': _L0_ffn_in['W3'], 'L0_ffn_b3': _L0_ffn_in['b3'], 'L0_ffn_A3': _L0_ffn_in['A3'], 'L0_ffn_B3': _L0_ffn_in['B3']}

def reference(x, ctx_1024, g_xattn, g_ffn, L0_xattn_Wq, L0_xattn_Wk, L0_xattn_Wv, L0_ffn_Wg, L0_ffn_W1, L0_ffn_b1, L0_ffn_A1, L0_ffn_B1, L0_ffn_W2, L0_ffn_b2, L0_ffn_A2, L0_ffn_B2, L0_ffn_W3, L0_ffn_b3, L0_ffn_A3, L0_ffn_B3):
    import jax
    import jax.numpy as jnp

    def _L0_xattn_ref(query, key, value, Wq, Wk, Wv):
        import jax, jax.numpy as jnp
        import numpy as np
        THETA = 10000.0
        SCALE_BASE = 512.0
        GAMMA = 0.96875

        def _dup_interleave(x):
            return jnp.repeat(x, 2, axis=-1)

        def _xpos(x, offset, inverse_scale):
            L, d = (x.shape[-2], x.shape[-1])
            half = d // 2
            base = (jnp.arange(0, d, 2, dtype=x.dtype) + 0.4 * d) / (1.4 * d)
            pos = jnp.arange(offset, offset + L, dtype=x.dtype)
            scale = base[None, :] ** (pos[:, None] / SCALE_BASE)
            freqs = 1.0 / THETA ** (jnp.arange(half, dtype=x.dtype) / half)
            sin_in = pos[:, None] * freqs[None, :]
            if inverse_scale:
                scale = 1.0 / scale
            sin = _dup_interleave(jnp.sin(sin_in) * scale)
            cos = _dup_interleave(jnp.cos(sin_in) * scale)
            rot = jnp.stack((-x[..., 1::2], x[..., ::2]), axis=-1).reshape(x.shape)
            return x * cos + rot * sin

        def _decay_mask(L, gamma, dtype):
            u = jnp.arange(L, dtype=dtype)[:, None]
            v = jnp.arange(L, dtype=dtype)[None, :]
            return jnp.where(u >= v, gamma ** (u - v), jnp.zeros((), dtype))
        q = jnp.einsum('ble,de->bld', query, Wq)
        k = jnp.einsum('ble,de->bld', key, Wk)
        v = jnp.einsum('ble,de->bld', value, Wv)
        q = _xpos(q, 0, False)
        k = _xpos(k, 0, True)
        L = q.shape[-2]
        mask = _decay_mask(L, jnp.asarray(GAMMA, q.dtype), q.dtype)
        retention = jnp.einsum('bqd,bkd->bqk', q, k) * mask[None, :, :]
        out = jnp.einsum('bqk,bkv->bqv', retention, v)
        return out

    def _L0_ffn_ref(x, Wg, W1, b1, A1, B1, W2, b2, A2, B2, W3, b3, A3, B3):
        import jax, jax.numpy as jnp
        import numpy as np
        DIM = 256
        HID = 512
        E = 8
        K = 2
        R = 16
        B_, S_ = (2, 256)

        def _lora_in(xf, W, b, A, B):
            base = jnp.einsum('td,ehd->teh', xf, W)
            low = jnp.einsum('ter,ehr->teh', jnp.einsum('td,erd->ter', xf, A), B)
            return base + low + b

        def _lora_out(g, W, b, A, B):
            base = jnp.einsum('teh,edh->ted', g, W)
            low = jnp.einsum('ter,edr->ted', jnp.einsum('teh,erh->ter', g, A), B)
            return base + low + b
        orig_shape = x.shape
        xf = x.reshape(-1, x.shape[-1])
        scores = jax.nn.softmax(xf @ Wg.T, axis=-1)
        expert_weights, expert_indices = jax.lax.top_k(scores, K)
        expert_weights = expert_weights / expert_weights.sum(-1, keepdims=True)
        gates = (jax.nn.one_hot(expert_indices, E, dtype=xf.dtype) * expert_weights[..., None]).sum(axis=1)
        h1 = _lora_in(xf, W1, b1, A1, B1)
        h3 = _lora_in(xf, W3, b3, A3, B3)
        g = jax.nn.silu(h1) * h3
        y_e = _lora_out(g, W2, b2, A2, B2)
        y = jnp.einsum('te,ted->td', gates, y_e)
        return y.reshape(orig_shape)
    x = x + jnp.tanh(g_xattn[0]) * _L0_xattn_ref(_layernorm(x, axis=-1), ctx_1024, ctx_1024, L0_xattn_Wq, L0_xattn_Wk, L0_xattn_Wv)
    x = x + jnp.tanh(g_ffn[0]) * _L0_ffn_ref(_layernorm(x, axis=-1), L0_ffn_Wg, L0_ffn_W1, L0_ffn_b1, L0_ffn_A1, L0_ffn_B1, L0_ffn_W2, L0_ffn_b2, L0_ffn_A2, L0_ffn_B2, L0_ffn_W3, L0_ffn_b3, L0_ffn_A3, L0_ffn_B3)
    return x

_drawn_inputs = setup_inputs


def setup_inputs(seed=0):
    import zlib

    import numpy as np

    out = dict(_drawn_inputs(seed))
    spreads = {'L0_ffn_b1': (0.0, 0.8), 'L0_ffn_b2': (0.0, 0.8), 'L0_ffn_b3': (0.0, 0.8)}
    factors = {'L0_ffn_Wg': 8.0,
     'L0_ffn_W1': 8.0,
     'L0_ffn_A1': 8.0,
     'L0_ffn_B1': 8.0,
     'L0_ffn_W2': 8.0,
     'L0_ffn_A2': 8.0,
     'L0_ffn_B2': 8.0,
     'L0_ffn_W3': 8.0,
     'L0_ffn_A3': 8.0,
     'L0_ffn_B3': 8.0}
    for name, (base, spread) in spreads.items():
        noise = np.random.default_rng([zlib.crc32(name.encode()), seed]).standard_normal(out[name].shape)
        drawn = base * np.exp(spread * noise) if base else spread * noise
        out[name] = jnp.asarray(drawn.astype(out[name].dtype))
    for name, factor in factors.items():
        out[name] = (out[name] * factor).astype(out[name].dtype)
    return out
```

```python
from contextlib import ExitStack

import numpy as np

import concourse.bass as bass
from concourse import mybir

F32 = mybir.dt.float32
F32R = mybir.dt.float32r
BF16 = mybir.dt.bfloat16
I32 = mybir.dt.int32
U32 = mybir.dt.uint32
ALU = mybir.AluOpType
ACT = mybir.ActivationFunctionType
AX = mybir.AxisListType.X

P = 128
B, S, D = 8, 256, 256
E, HID, R, K = 8, 512, 16, 2
TOK = B * S
NJ = TOK // P
CH = D // P
HC = HID // P
TPB = S // P
NT_SLOTS = TOK * K // P + E - 1
KJ = K * NJ
EPS = 1e-5
GAMMA = 0.96875
KINDS = 3
WCOL = CH * HID
UNITS = 2 * KINDS
UC = WCOL // 2
LCOL = D + HID
LROWS = 3 * 32
BCOL = 2 * HID + D

C_TRI, C_IOTA, C_SEG = 0, P, 2 * P
C_HI = 3 * P
C_TILE = C_HI + KJ
C_E = C_TILE + NT_SLOTS
C_P = C_E + E
C_PAD = C_P + 1
C_END = C_PAD + 1


def flamingo(nc, x, ctxT, wqkv, tables, mask, gates_in, w_all, lora, biases, wgT, ident_in, consts, out):
    xn2_d = nc.dram_tensor("xn2_rows", (TOK, D), F32, kind="Internal").ap()
    x2_d = nc.dram_tensor("x2_rows", (TOK, D), F32, kind="Internal").ap()
    y_d = nc.dram_tensor("y_rows", (K * TOK, D), F32, kind="Internal").ap()

    whole = ExitStack()
    with whole:
        def sb(stack, name, shape, dt=F32):
            return stack.enter_context(nc.sbuf_tensor(name, shape, dt))

        def sem(name):
            return whole.enter_context(nc.semaphore(name))

        bank = [whole.enter_context(nc.psum_tensor(f"bank{i}", [P, 512], F32)) for i in range(8)]

        WH = sb(whole, "WH", [P, E * KINDS * WCOL], F32R)
        WL = sb(whole, "WL", [P, E * KINDS * WCOL], BF16)
        ident = sb(whole, "ident", [P, P])
        cst = sb(whole, "cst", [P, C_END])
        tg = sb(whole, "tg", [P, 2])
        M2 = sb(whole, "M2", [P, NJ, K])
        I2 = sb(whole, "I2", [P, NJ, K])

        early = ExitStack()
        tab = sb(early, "tab", [P, 4, S])
        msk = sb(early, "msk", [P, 3 * P])
        wq = sb(early, "wq", [P, 3, CH, D])
        wg = sb(early, "wg", [P, CH, E])
        gin = sb(early, "gin", [P, 2])
        eps_t = sb(early, "eps_t", [P, 1])
        xs = [sb(early, f"xs{p}", [P, TPB, D]) for p in range(2)]
        x2 = [sb(early, f"x2_{p}", [P, TPB, D]) for p in range(2)]
        cx = [sb(early, f"cx{p}", [P, CH, S]) for p in range(2)]
        xn = sb(early, "xn", [P, TPB, D])
        xnT = sb(early, "xnT", [P, CH, S])
        xn2 = [sb(early, f"xn2_{p}", [P, TPB, D]) for p in range(2)]
        xn2T = sb(early, "xn2T", [P, CH, S])
        qT = sb(early, "qT", [P, 2, S])
        kT = sb(early, "kT", [P, 2, S])
        v = [sb(early, f"v{p}", [P, TPB, D]) for p in range(2)]
        ret = sb(early, "ret", [P, 3 * P])
        tA = sb(early, "tA", [P, 2, S])
        tB = sb(early, "tB", [P, 2, S])
        stage = [sb(early, f"stage{i}", [P, UC]) for i in range(3)]
        LR = sb(early, "LR", [LROWS, LCOL])
        LS = sb(early, "LS", [LROWS, LCOL], F32R)
        st1 = sb(early, "st1", [P, TPB, 6]); mv1 = sb(early, "mv1", [P, TPB, 2])
        sd1 = sb(early, "sd1", [P, TPB]); rs1 = sb(early, "rs1", [P, TPB])
        st2 = sb(early, "st2", [P, TPB, 6]); mv2 = sb(early, "mv2", [P, TPB, 2])
        sd2 = sb(early, "sd2", [P, TPB]); rs2 = sb(early, "rs2", [P, TPB])
        L8 = sb(early, "L8", [P, TPB, E])
        M8 = sb(early, "M8", [P, TPB, 8])
        I8 = sb(early, "I8", [P, TPB, 8], U32)
        early.close()

        SEL = sb(whole, "SEL", [LROWS, E, P], BF16)
        B3 = sb(whole, "B3", [LROWS, BCOL], BF16)
        X2 = sb(whole, "X2", [P, NJ, D])
        gate = sb(whole, "gate", [P, K, NJ])
        gidx = sb(whole, "gidx", [P, NT_SLOTS], U32)
        sidx = sb(whole, "sidx", [P, NT_SLOTS], U32)
        eid = sb(whole, "eid", [1, NT_SLOTS], I32)
        route = ExitStack()
        braw = sb(route, "braw", [LROWS, BCOL]); bmid = sb(route, "bmid", [LROWS, BCOL], BF16)
        bhi = sb(route, "bhi", [LROWS, BCOL], BF16)
        tri = sb(route, "tri", [P, P], BF16); ones = sb(route, "ones", [P, P], BF16)
        idxf = sb(route, "idxf", [P, K, NJ])
        OH = sb(route, "OH", [P, K, E, NJ], BF16); H = sb(route, "H", [P, E, NJ], BF16)
        CNT = sb(route, "CNT", [P, E, NJ]); INC = sb(route, "INC", [P, E, NJ])
        ti = sb(route, "ti", [P, E], I32); ts = sb(route, "ts", [P, E], I32)
        nt = sb(route, "nt", [P, E]); tend = sb(route, "tend", [P, E]); base = sb(route, "base", [P, E])
        one8 = sb(route, "one8", [P, E])
        Z = sb(route, "Z", [P, E, NJ]); PO = sb(route, "PO", [P, E, NJ])
        PK = sb(route, "PK", [P, K, E, NJ]); pos = sb(route, "pos", [P, K, NJ])
        posi = sb(route, "posi", [P, KJ], I32); sli = sb(route, "sli", [P, KJ], I32)
        tli = sb(route, "tli", [P, KJ], I32)
        slf = sb(route, "slf", [P, KJ]); tlf = sb(route, "tlf", [P, KJ])
        AT = sb(route, "AT", [P, KJ, 3, NT_SLOTS], BF16)
        BS = sb(route, "BS", [P, KJ, P], BF16)
        SV = sb(route, "SV", [P, 3, NT_SLOTS]); val = sb(route, "val", [P, NT_SLOTS])
        gof = sb(route, "gof", [P, NT_SLOTS]); nh = sb(route, "nh", [P, NT_SLOTS])
        ET = sb(route, "ET", [1, NT_SLOTS, E]); ef = sb(route, "ef", [1, NT_SLOTS])
        dl = sb(route, "dl", [P, NJ]); e2 = sb(route, "e2", [P, NJ]); den = sb(route, "den", [P, NJ])
        wa = sb(route, "wa", [P, NJ]); wb = sb(route, "wb", [P, NJ])
        route.close()
        tiles = ExitStack()
        gi = [sb(tiles, f"gi{p}", [P, 1], U32) for p in range(2)]
        si = [sb(tiles, f"si{p}", [P, 1], U32) for p in range(2)]
        xg = [sb(tiles, f"xg{p}", [P, D]) for p in range(2)]
        xh = [sb(tiles, f"xh{p}", [P, D], F32R) for p in range(2)]
        xl = [sb(tiles, f"xl{p}", [P, D], F32R) for p in range(2)]
        xb = [sb(tiles, f"xb{p}", [P, D], BF16) for p in range(2)]
        sl = sb(tiles, "sl", [P, HID]); g = sb(tiles, "g", [P, HID])
        gh = sb(tiles, "gh", [P, HID], F32R); gl = sb(tiles, "gl", [P, HID], F32R)
        gb = sb(tiles, "gb", [P, HID], BF16)
        ys = [sb(tiles, f"ys{p}", [P, D]) for p in range(2)]
        yk = [[sb(tiles, f"yk{p}{k}", [P, TPB, D]) for k in range(K)] for p in range(2)]
        tiles.close()

        s_waited = sem("s_waited")
        s_tab, s_gin, s_cst = sem("s_tab"), sem("s_gin"), sem("s_cst")
        s_xload, s_ctx = [sem(f"s_xload{p}") for p in range(2)], [sem(f"s_ctx{p}") for p in range(2)]
        s_stage = [sem(f"s_stage{i}") for i in range(3)]
        s_lraw, s_lzero = sem("s_lraw"), sem("s_lzero")
        s_store = sem("s_store")
        s_eps, s_tg = sem("s_eps"), sem("s_tg")
        s_lhi, s_lfix = sem("s_lhi"), sem("s_lfix")
        s_unit, s_add, s_wh, s_wl = sem("s_unit"), sem("s_add"), sem("s_wh"), sem("s_wl")
        s_kproj, s_vproj, s_qproj = sem("s_kproj"), sem("s_vproj"), sem("s_qproj")
        s_krot, s_qrot, s_kT, s_qT, s_v = sem("s_krot"), sem("s_qrot"), sem("s_kT"), sem("s_qT"), sem("s_v")
        s_scores, s_ret, s_out, s_x2 = sem("s_scores"), sem("s_ret"), sem("s_out"), sem("s_x2")
        s_mv1, s_sd1, s_xn, s_xnTp, s_xnT = sem("s_mv1"), sem("s_sd1"), sem("s_xn"), sem("s_xnTp"), sem("s_xnT")
        s_mv2, s_sd2, s_xn2, s_xn2Tp, s_xn2T = (sem("s_mv2"), sem("s_sd2"), sem("s_xn2"), sem("s_xn2Tp"),
                                                 sem("s_xn2T"))
        s_logit, s_L = sem("s_logit"), sem("s_L")
        s_ln = sem("s_ln")
        s_top, s_two = sem("s_top"), sem("s_two")
        s_r = sem("s_r")
        s_braw, s_bzero, s_b = sem("s_braw"), sem("s_bzero"), sem("s_b")
        s_H, s_rank, s_at, s_slots = sem("s_H"), sem("s_rank"), sem("s_at"), sem("s_slots")
        s_routed, s_e2, s_dl = sem("s_routed"), sem("s_e2"), sem("s_dl")
        s_X2 = sem("s_X2")
        s_gi, s_si = sem("s_gi"), sem("s_si")
        s_xg = [sem(f"s_xg{p}") for p in range(2)]
        s_xT, s_xh, s_xl, s_xb = sem("s_xT"), sem("s_xh"), sem("s_xl"), sem("s_xb")
        s_h1, s_h3, s_silu, s_g = sem("s_h1"), sem("s_h3"), sem("s_silu"), sem("s_g")
        s_gT, s_gh, s_gl, s_gb = sem("s_gT"), sem("s_gh"), sem("s_gl"), sem("s_gb")
        s_y, s_ys = sem("s_y"), sem("s_ys")
        s_scat = [sem(f"s_scat{p}") for p in range(2)]
        s_yk = [sem(f"s_yk{p}") for p in range(2)]
        s_sum, s_fin = sem("s_sum"), sem("s_fin")
        s_outd = sem("s_outd")

        block = whole.enter_context(nc.Block())

        pK, pQ, pV, pT, pS, pO, pW, pL = bank

        def batch_steps(engine, step):
            for s in (0, 1):
                step(s, s % 2, True, s >= 1, False)
            with engine.Fori(1, B // 2) as r:
                for u in range(2):
                    step(2 * r + u, u, True, True, True)
            step(B, 0, False, True, True)
            step(B + 1, 1, False, False, True)

        def half(s, u):
            return (s - u) // 2

        def pos_wait(eng, sm, val):
            if not isinstance(val, int) or val > 0:
                eng.wait_ge(sm, val)

        def settle(eng):
            eng.sem_inc(s_waited, 1)

        w_dst = lambda t, e, m: t[:, bass.ds((e * UNITS + m) * UC, UC)]

        @block.sync
        def _(sp):
            sp.dma_start(wq[:], wqkv).then_inc(s_tab, 16)
            sp.dma_start(tab[:], tables).then_inc(s_tab, 16)
            sp.dma_start(msk[:], mask).then_inc(s_tab, 16)
            sp.dma_start(wg[:], wgT).then_inc(s_tab, 16)
            sp.dma_start(ident[:], ident_in).then_inc(s_tab, 16)
            sp.dma_start(gin[:], gates_in).then_inc(s_gin, 16)
            sp.dma_start(cst[:], consts).then_inc(s_cst, 16)
            sp.wait_ge(s_lzero, 1)

            def step(s, u, one, two, three):
                if one:
                    pos_wait(sp, s_vproj, s - 1)
                    settle(sp)
                    sp.dma_start(cx[u][:], ctxT[s]).then_inc(s_ctx[u], 16)
                    pos_wait(sp, s_x2, s - 1)
                    settle(sp)
                    sp.dma_start(xs[u][:], x[s]).then_inc(s_xload[u], 16)
                    for m in range(UNITS):
                        n = s * UNITS + m
                        if m % 2 == 0:
                            i = s * KINDS + m // 2
                            pos_wait(sp, s_lfix, 2 * i)
                            settle(sp)
                            for slot in range(3):
                                sp.dma_start(LR[32 * slot:32 * slot + R, :], lora[s, m // 2]).then_inc(s_lraw, 16)
                        pos_wait(sp, s_wl, n - 2)
                        settle(sp)
                        sp.dma_start(stage[m % 3][:], w_all[s, m]).then_inc(s_stage[m % 3], 16)
                if three:
                    b = s - 2
                    sp.wait_ge(s_x2, b + 1)
                    settle(sp)
                    sp.dma_start(x2_d[bass.ds(b * S, S), :].rearrange("(t p) d -> p t d", p=P), x2[u][:]).then_inc(s_store, 16)
                    sp.wait_ge(s_xn2, b + 1)
                    settle(sp)
                    sp.dma_start(xn2_d[bass.ds(b * S, S), :].rearrange("(t p) d -> p t d", p=P), xn2[u][:]).then_inc(s_store, 16)
                    sp.wait_ge(s_store, 32 * (b + 1))
                    settle(sp)

            batch_steps(sp, step)
            sp.wait_ge(s_wl, E * UNITS)
            sp.wait_ge(s_L, B)
            sp.wait_ge(s_bzero, 1)
            for slot in range(3):
                sp.dma_start(braw[32 * slot:32 * slot + E, :], biases).then_inc(s_braw, 16)
            sp.dma_start(X2[:], x2_d.rearrange("(j p) d -> p j d", p=P)).then_inc(s_X2, 16)

            sp.wait_ge(s_scat[0], 16 * ((NT_SLOTS + 1) // 2))
            sp.wait_ge(s_scat[1], 16 * (NT_SLOTS // 2))

            def load(b, p):
                for k in range(K):
                    sp.dma_start(yk[p][k][:], y_d[bass.ds(k * TOK + b * S, S), :].rearrange("(t p) d -> p t d", p=P)
                                 ).then_inc(s_yk[p], 16)

            def store(b):
                sp.wait_ge(s_fin, b + 1)
                settle(sp)
                sp.dma_start(out[b].rearrange("(t p) d -> p t d", p=P), X2[:, bass.ds(b * TPB, TPB), :]).then_inc(s_outd, 16)

            load(0, 0)
            load(1, 1)
            with sp.Fori(0, B // 2 - 1) as r:
                for p in range(2):
                    store(2 * r + p)
                    load(2 * r + p + 2, p)
            store(B - 2)
            store(B - 1)
            sp.wait_ge(s_outd, 16 * B)

        @block.tensor
        def _(pe):
            pe.wait_ge(s_tab, 5 * 16)

            def unit(s, m):
                kind, n = m // 2, s * UNITS + m
                if m % 2 == 0:
                    pe.wait_ge(s_lfix, 2 * (s * KINDS + kind + 1))
                pos_wait(pe, s_add, n)
                if kind < 2:
                    c = m % 2
                    last = nc.tensor.matmul(pW[:, :], LS[:, c * P:(c + 1) * P], LS[:, D:LCOL], start=True, stop=True)
                else:
                    for i in range(2):
                        c = 2 * (m % 2) + i
                        last = nc.tensor.matmul(pW[:, i * D:(i + 1) * D], LS[:, c * P:(c + 1) * P], LS[:, HID:LCOL],
                                                start=True, stop=True)
                last.then_inc(s_unit, 1)

            def transposes(src, sig):
                for t in range(TPB):
                    for c in range(CH):
                        last = nc.tensor.transpose(pT[:, c * S + t * P:c * S + (t + 1) * P], src[:, t, c * P:(c + 1) * P],
                                                   ident[:])
                last.then_inc(sig, 1)

            def step(s, u, one, two, three):
                if one:
                    pe.wait_ge(s_ctx[u], 16 * (half(s, u) + 1))
                    pos_wait(pe, s_krot, s)
                    for m in range(2):
                        for c in range(CH):
                            last = nc.tensor.matmul(pK[:, m * S:(m + 1) * S], wq[:, 1, c, m * P:(m + 1) * P], cx[u][:, c, :],
                                                    start=(c == 0), stop=(c == CH - 1))
                    last.then_inc(s_kproj, 1)
                if two:
                    pe.wait_ge(s_kT, 2 * s)
                    pe.wait_ge(s_qT, 2 * s)
                    for kb in range(TPB):
                        o, n = kb * S, S - kb * P
                        for m in range(2):
                            last = nc.tensor.matmul(pS[:, o:o + n], kT[:, m, kb * P:(kb + 1) * P], qT[:, m, kb * P:S],
                                                    start=(m == 0), stop=(m == 1))
                    last.then_inc(s_scores, 1)
                if one:
                    unit(s, 0)
                    pos_wait(pe, s_v, s)
                    for t in range(TPB):
                        for c in range(CH):
                            last = nc.tensor.matmul(pV[:, t * D:(t + 1) * D], cx[u][:, c, t * P:(t + 1) * P], wq[:, 2, c, :],
                                                    start=(c == 0), stop=(c == CH - 1))
                    last.then_inc(s_vproj, 1)
                    unit(s, 1)
                if two:
                    vv = v[1 - u]
                    pe.wait_ge(s_ret, s)
                    pe.wait_ge(s_v, s)
                    pos_wait(pe, s_x2, s - 1)
                    nc.tensor.matmul(pO[:, 0:D], ret[:, 0:P], vv[:, 0, :], start=True, stop=True)
                    nc.tensor.matmul(pO[:, D:2 * D], ret[:, P:2 * P], vv[:, 0, :], start=True, stop=False)
                    nc.tensor.matmul(pO[:, D:2 * D], ret[:, 2 * P:3 * P], vv[:, 1, :], start=False, stop=True
                                     ).then_inc(s_out, 1)
                if one:
                    pe.wait_ge(s_xn, s + 1)
                    transposes(xn, s_xnTp)
                    unit(s, 2)
                    pe.wait_ge(s_xnT, s + 1)
                if three:
                    pe.wait_ge(s_xn2, s - 1)
                    transposes(xn2[u], s_xn2Tp)
                if one:
                    unit(s, 3)
                    for m in range(2):
                        for c in range(CH):
                            last = nc.tensor.matmul(pQ[:, m * S:(m + 1) * S], wq[:, 0, c, m * P:(m + 1) * P], xnT[:, c, :],
                                                    start=(c == 0), stop=(c == CH - 1))
                    last.then_inc(s_qproj, 1)
                    unit(s, 4)
                if three:
                    pe.wait_ge(s_xn2T, s - 1)
                    if not one:
                        pe.wait_ge(s_L, s - 2)
                    for t in range(TPB):
                        for c in range(CH):
                            last = nc.tensor.matmul(pL[:, t * E:(t + 1) * E], xn2T[:, c, t * P:(t + 1) * P], wg[:, c, :],
                                                    start=(c == 0), stop=(c == CH - 1))
                    last.then_inc(s_logit, 1)
                if one:
                    unit(s, 5)

            batch_steps(pe, step)

            Hf = H[:].rearrange("p e j -> p (e j)")
            pe.wait_ge(s_H, 1)
            nc.tensor.matmul(pK[:, 0:P], tri[:], Hf, start=True, stop=True)
            nc.tensor.matmul(pQ[:, 0:P], ones[:], Hf, start=True, stop=True).then_inc(s_rank, 1)
            for kj in range(KJ):
                if kj % (KJ // 4) == 0:
                    pe.wait_ge(s_at, kj // (KJ // 4) + 1)
                last = nc.tensor.matmul(pV[:, 0:3 * NT_SLOTS], BS[:, kj, :], AT[:, kj].rearrange("p a i -> p (a i)"),
                                        start=(kj == 0), stop=(kj == KJ - 1))
            last.then_inc(s_slots, 1)

            pX, pH1, pH3, pG, pY = bank[0], bank[1], bank[2], bank[3], bank[4]

            def x_transposes(i, p):
                pe.wait_ge(s_xg[p], 16 * (half(i, p) + 1))
                if not isinstance(i, int) or i > 0:
                    pe.wait_ge(s_xh, i)
                    pe.wait_ge(s_xb, i)
                    pe.wait_ge(s_xl, i)
                for c in range(CH):
                    last = nc.tensor.transpose(pX[:, c * P:(c + 1) * P], xg[p][:, c * P:(c + 1) * P], ident[:])
                last.then_inc(s_xT, 1)

            def up(dst, i, p, e, kind, sig):
                if kind == 0:
                    pos_wait(pe, s_silu, i)
                nc.tensor.matmul(dst[:, :], SEL[:].rearrange("p e q -> p (e q)")[:, bass.ds(e * P, P)],
                                 B3[:, kind * HID:(kind + 1) * HID], start=True, stop=False)
                for part, (lhs, W, ready) in enumerate(((xh, WH, s_xh), (xl, WH, s_xl), (xb, WL, s_xb))):
                    if kind == 0:
                        pe.wait_ge(ready, i + 1)
                    for c in range(CH):
                        last = nc.tensor.matmul(dst[:, :], lhs[p][:, c * P:(c + 1) * P],
                                                W[:, bass.ds(e * (UNITS * UC) + (2 * kind + c) * UC, HID)],
                                                start=False, stop=(part == 2 and c == CH - 1))
                last.then_inc(sig, 1)

            def g_transposes(i):
                pe.wait_ge(s_g, i + 1)
                for c in range(HC):
                    last = nc.tensor.transpose(pG[:, c * P:(c + 1) * P], g[:, c * P:(c + 1) * P], ident[:])
                last.then_inc(s_gT, 1)

            def down(i, e):
                pos_wait(pe, s_ys, i)
                nc.tensor.matmul(pY[:, 0:D], SEL[:].rearrange("p e q -> p (e q)")[:, bass.ds(e * P, P)], B3[:, 2 * HID:BCOL],
                                 start=True, stop=False)
                for part, (lhs, W, ready) in enumerate(((gh, WH, s_gh), (gl, WH, s_gl), (gb, WL, s_gb))):
                    pe.wait_ge(ready, i + 1)
                    for c in range(HC):
                        last = nc.tensor.matmul(pY[:, 0:D], lhs[:, c * P:(c + 1) * P],
                                                W[:, bass.ds(e * (UNITS * UC) + 4 * UC + c * D, D)],
                                                start=False, stop=(part == 2 and c == HC - 1))
                last.then_inc(s_y, 1)

            def expert(i):
                return pe.value_load(eid[0:1, bass.ds(i, 1)], min_val=0, max_val=E - 1)

            def tile(i, p, first, more):
                if more:
                    x_transposes(i + 1, 1 - p)
                e = expert(i)
                up(pH1, i, p, e, 0, s_h1)
                if not first:
                    g_transposes(i - 1)
                up(pH3, i, p, e, 1, s_h3)
                if not first:
                    down(i - 1, expert(i - 1))

            pe.wait_ge(s_routed, 1)
            pe.wait_ge(s_b, 1)
            x_transposes(0, 0)
            tile(0, 0, True, True)
            with pe.Fori(0, (NT_SLOTS - 3) // 2) as r:
                for p in range(2):
                    tile(2 * r + 1 + p, 1 - p, False, True)
            tile(NT_SLOTS - 2, 1, False, True)
            tile(NT_SLOTS - 1, 0, False, False)
            g_transposes(NT_SLOTS - 1)
            down(NT_SLOTS - 1, expert(NT_SLOTS - 1))

        @block.scalar
        def _(act):
            act.wait_ge(s_gin, 16)
            nc.scalar.activation(tg[:], gin[:], ACT.Tanh).then_inc(s_tg, 1)
            act.wait_ge(s_eps, 1)

            def lora_hi(s, kind):
                i = s * KINDS + kind
                act.wait_ge(s_lraw, 48 * (i + 1))
                pos_wait(act, s_unit, 2 * i)
                nc.scalar.activation(LS[:, :], LR[:, :], ACT.Copy).then_inc(s_lhi, 1)

            def weight_hi(s, m):
                act.wait_ge(s_add, s * UNITS + m + 1)
                nc.scalar.activation(w_dst(WH, s, m), stage[m % 3][:], ACT.Copy).then_inc(s_wh, 1)

            def step(s, u, one, two, three):
                if one:
                    lora_hi(s, 0)
                    act.wait_ge(s_mv1, s + 1)
                    nc.scalar.activation(sd1[:], mv1[:, :, 1], ACT.Sqrt, bias=eps_t[:]).then_inc(s_sd1, 1)
                    act.wait_ge(s_vproj, s + 1)
                    pos_wait(act, s_out, s - 1)
                    nc.scalar.activation(v[u][:].rearrange("p t d -> p (t d)"), pV[:, :], ACT.Copy).then_inc(s_v, 1)
                    weight_hi(s, 0)
                    weight_hi(s, 1)
                    lora_hi(s, 1)
                    act.wait_ge(s_xnTp, s + 1)
                    pos_wait(act, s_qproj, s)
                    nc.scalar.activation(xnT[:].rearrange("p c t -> p (c t)"), pT[:, :], ACT.Copy).then_inc(s_xnT, 1)
                if two:
                    act.wait_ge(s_mv2, s)
                    nc.scalar.activation(sd2[:], mv2[:, :, 1], ACT.Sqrt, bias=eps_t[:]).then_inc(s_sd2, 1)
                if three:
                    act.wait_ge(s_xn2Tp, s - 1)
                    nc.scalar.activation(xn2T[:].rearrange("p c t -> p (c t)"), pT[:, :], ACT.Copy).then_inc(s_xn2T, 1)
                if one:
                    weight_hi(s, 2)
                    weight_hi(s, 3)
                    lora_hi(s, 2)
                    weight_hi(s, 4)
                    weight_hi(s, 5)

            batch_steps(act, step)
            act.wait_ge(s_dl, 1)
            nc.scalar.activation(e2[:], dl[:], ACT.Exp).then_inc(s_e2, 1)

            pX, pH1, pG = bank[0], bank[1], bank[3]

            def x_parts(i, p):
                act.wait_ge(s_xT, i + 1)
                pos_wait(act, s_h3, i - 1)
                nc.scalar.activation(xh[p][:], pX[:, 0:D], ACT.Copy).then_inc(s_xh, 1)
                nc.scalar.activation(xb[p][:], pX[:, 0:D], ACT.Copy).then_inc(s_xb, 1)

            def g_parts(i):
                act.wait_ge(s_gT, i + 1)
                pos_wait(act, s_y, i)
                nc.scalar.activation(gh[:], pG[:, :], ACT.Copy).then_inc(s_gh, 1)
                act.wait_ge(s_gh, i + 1)
                nc.scalar.activation(gb[:], gh[:].bitcast(F32), ACT.Copy).then_inc(s_gb, 1)

            def tile(i, p, first, more):
                if more:
                    x_parts(i + 1, 1 - p)
                if not first:
                    g_parts(i - 1)
                act.wait_ge(s_h1, i + 1)
                pos_wait(act, s_g, i)
                nc.scalar.activation(sl[:], pH1[:, :], ACT.Silu).then_inc(s_silu, 1)

            act.wait_ge(s_routed, 1)
            x_parts(0, 0)
            tile(0, 0, True, True)
            with act.Fori(0, (NT_SLOTS - 3) // 2) as r:
                for p in range(2):
                    tile(2 * r + 1 + p, 1 - p, False, True)
            tile(NT_SLOTS - 2, 1, False, True)
            tile(NT_SLOTS - 1, 0, False, False)
            g_parts(NT_SLOTS - 1)

        @block.gpsimd
        def _(pool):
            nc.gpsimd.memset(LR[:, :], 0.0).then_inc(s_lzero, 1)
            nc.gpsimd.memset(eps_t[:], EPS).then_inc(s_eps, 1)

            def lora_lo(s, kind):
                i = s * KINDS + kind
                a = D if kind < 2 else HID
                pool.wait_ge(s_lhi, i + 1)
                pos_wait(pool, s_wl, s * UNITS + 2 * kind)
                for n, (rows, c0, c1) in enumerate(((32, 0, a), (64, a, LCOL))):
                    part = (slice(rows, rows + R), slice(c0, c1))
                    nc.gpsimd.tensor_tensor(LS[part], LR[part], LS[part].bitcast(F32), ALU.subtract).then_inc(s_lfix, 1)
                    pool.wait_ge(s_lfix, 2 * i + n + 1)

            def weight_lo(s, m):
                pool.wait_ge(s_wh, s * UNITS + m + 1)
                nc.gpsimd.tensor_tensor(w_dst(WL, s, m), stage[m % 3][:], w_dst(WH, s, m).bitcast(F32),
                                        ALU.subtract).then_inc(s_wl, 1)

            def rotated(dst, sig):
                nc.gpsimd.tensor_tensor(dst[:, 0, :], tA[:, 0, :], tB[:, 1, :], ALU.subtract).then_inc(sig, 1)
                nc.gpsimd.tensor_tensor(dst[:, 1, :], tA[:, 1, :], tB[:, 0, :], ALU.add).then_inc(sig, 1)

            def step(s, u, one, two, three):
                if one:
                    lora_lo(s, 0)
                    pool.wait_ge(s_krot, s + 1)
                    if two:
                        pool.wait_ge(s_scores, s)
                    rotated(kT, s_kT)
                    weight_lo(s, 0)
                    weight_lo(s, 1)
                    lora_lo(s, 1)
                    weight_lo(s, 2)
                    weight_lo(s, 3)
                    lora_lo(s, 2)
                    pool.wait_ge(s_qrot, s + 1)
                    rotated(qT, s_qT)
                    weight_lo(s, 4)
                    weight_lo(s, 5)

            batch_steps(pool, step)

            pool.wait_ge(s_L, B)
            pool.wait_ge(s_store, 32 * B)
            nc.gpsimd.memset(braw[:, :], 0.0).then_inc(s_bzero, 1)
            nc.gpsimd.memset(SEL[:], 0.0).then_inc(s_bzero, 1)
            pool.wait_ge(s_bzero, 2)
            for slot in range(3):
                part = SEL[32 * slot:32 * slot + E, :, :]
                nc.gpsimd.affine_select(out=part, in_=part, compare_op=ALU.not_equal, fill=1.0, base=0,
                                        pattern=[[-1, E], [0, P]], channel_multiplier=1).then_inc(s_bzero, 1)
            pool.wait_ge(s_bzero, 5)
            pool.wait_ge(s_braw, 48)
            nc.gpsimd.tensor_copy(bhi[:], braw[:]).then_inc(s_bzero, 1)
            nc.gpsimd.tensor_copy(B3[:], braw[:]).then_inc(s_bzero, 1)
            pool.wait_ge(s_bzero, 7)
            nc.gpsimd.tensor_tensor(braw[:], braw[:], bhi[:], ALU.subtract).then_inc(s_bzero, 1)
            pool.wait_ge(s_bzero, 8)
            nc.gpsimd.tensor_copy(bmid[:], braw[:]).then_inc(s_bzero, 1)
            pool.wait_ge(s_bzero, 9)
            nc.gpsimd.tensor_copy(B3[32:64, :], braw[32:64, :]).then_inc(s_bzero, 1)
            pool.wait_ge(s_bzero, 10)
            nc.gpsimd.tensor_tensor(B3[64:96, :], braw[64:96, :], bmid[64:96, :], ALU.subtract).then_inc(s_b, 1)
            pool.wait_ge(s_b, 1)

            def gather(i, p):
                pos_wait(pool, s_xT, i - 1)
                nc.gpsimd.tensor_copy(gi[p][:], gidx[:, bass.ds(i, 1)]).then_inc(s_gi, 1)
                pool.wait_ge(s_gi, i + 1)
                settle(pool)
                nc.gpsimd.indirect_dma_start(out=xg[p][:], out_offset=None, in_=xn2_d,
                                             in_offset=bass.IndirectOffsetOnAxis(ap=gi[p][:, 0:1], axis=0)
                                             ).then_inc(s_xg[p], 16)

            def scatter(i, p):
                if not isinstance(i, int) or i >= 2:
                    pool.wait_ge(s_scat[p], 16 * half(i, p))
                nc.gpsimd.tensor_copy(si[p][:], sidx[:, bass.ds(i, 1)]).then_inc(s_si, 1)
                pool.wait_ge(s_si, i + 1)
                pool.wait_ge(s_ys, i + 1)
                settle(pool)
                nc.gpsimd.indirect_dma_start(out=y_d, out_offset=bass.IndirectOffsetOnAxis(ap=si[p][:, 0:1], axis=0),
                                             in_=ys[p][:], in_offset=None, bounds_check=K * TOK - 1,
                                             oob_is_err=False).then_inc(s_scat[p], 16)

            pool.wait_ge(s_routed, 1)
            gather(0, 0)
            gather(1, 1)
            for i in range(2):
                gather(i + 2, i)
                scatter(i, i)
            with pool.Fori(1, (NT_SLOTS - 3) // 2) as r:
                for p in range(2):
                    gather(2 * r + 2 + p, p)
                    scatter(2 * r + p, p)
            gather(NT_SLOTS - 1, 0)
            scatter(NT_SLOTS - 3, 0)
            scatter(NT_SLOTS - 2, 1)
            scatter(NT_SLOTS - 1, 0)

        @block.vector
        def _(dve):
            dve.wait_ge(s_tab, 5 * 16)
            dve.wait_ge(s_tg, 1)
            dve.wait_ge(s_cst, 16)

            def add(s, m):
                n = s * UNITS + m
                dve.wait_ge(s_unit, n + 1)
                dve.wait_ge(s_stage[m % 3], 16 * (2 * s + m // 3 + 1))
                nc.vector.tensor_tensor(stage[m % 3][:], pW[:, :], stage[m % 3][:], ALU.add).then_inc(s_add, 1)

            def rotate(bankt, which, sig):
                for dst, row in ((tA, 0), (tB, 1)):
                    t = tab[:, which + row, :].unsqueeze(1).to_broadcast([P, 2, S])
                    last = nc.vector.tensor_tensor(dst[:], bankt[:, :].rearrange("p (m t) -> p m t", m=2), t, ALU.mult)
                last.then_inc(sig, 1)

            def stats(src, st, mv, sig, n):
                for t in range(TPB):
                    last = nc.vector.bn_stats(st[:, t, :], src[:, t, :])
                last.then_inc(s_ln, 1)
                dve.wait_ge(s_ln, n + 1)
                settle(dve)
                for t in range(TPB):
                    last = nc.vector.bn_aggr(mv[:, t, :], st[:, t, :])
                last.then_inc(sig, 1)

            def normal(src, mv, sd, rs, dst, sig, n):
                nc.vector.reciprocal(rs[:], sd[:]).then_inc(s_ln, 1)
                dve.wait_ge(s_ln, n + 1)
                for t in range(TPB):
                    last = nc.vector.tensor_scalar(dst[:, t, :], src[:, t, :], mv[:, t, 0:1], rs[:, t:t + 1],
                                                   ALU.subtract, ALU.mult)
                last.then_inc(sig, 1)

            def step(s, u, one, two, three):
                ln = 4 * s - 2 if not isinstance(s, int) else (0 if s == 0 else 4 * s - 2)
                if not one:
                    ln = 4 * B - 2
                if one:
                    dve.wait_ge(s_kproj, s + 1)
                    pos_wait(dve, s_qT, 2 * s)
                    rotate(pK, 2, s_krot)
                if two:
                    dve.wait_ge(s_scores, s)
                    pos_wait(dve, s_out, s - 1)
                    nc.vector.tensor_tensor(ret[:], pS[:, 0:3 * P], msk[:], ALU.mult).then_inc(s_ret, 1)
                if one:
                    dve.wait_ge(s_xload[u], 16 * (half(s, u) + 1))
                    stats(xs[u], st1, mv1, s_mv1, ln)
                    add(s, 0)
                    dve.wait_ge(s_sd1, s + 1)
                    pos_wait(dve, s_xnTp, s)
                    normal(xs[u], mv1, sd1, rs1, xn, s_xn, ln + 1)
                    add(s, 1)
                    ln = ln + 2
                if two:
                    q = 1 - u
                    if not one:
                        dve.wait_ge(s_store, 32 * (s - 2))
                    dve.wait_ge(s_out, s)
                    nc.vector.scalar_tensor_tensor(x2[q][:].rearrange("p t d -> p (t d)"), pO[:, :], tg[:, 0:1],
                                                   xs[q][:].rearrange("p t d -> p (t d)"), ALU.mult, ALU.add
                                                   ).then_inc(s_x2, 1)
                    dve.wait_ge(s_x2, s)
                    stats(x2[q], st2, mv2, s_mv2, ln)
                    if one:
                        add(s, 2)
                    dve.wait_ge(s_sd2, s)
                    normal(x2[q], mv2, sd2, rs2, xn2[q], s_xn2, ln + 1)
                elif one:
                    add(s, 2)
                if one:
                    add(s, 3)
                    dve.wait_ge(s_qproj, s + 1)
                    dve.wait_ge(s_kT, 2 * (s + 1))
                    rotate(pQ, 0, s_qrot)
                    add(s, 4)
                if three:
                    b = s - 2
                    dve.wait_ge(s_logit, b + 1)
                    nc.vector.tensor_copy(L8[:], pL[:, 0:TPB * E].rearrange("p (t e) -> p t e", t=TPB)).then_inc(s_L, 1)
                    dve.wait_ge(s_L, b + 1)
                    settle(dve)
                    for t in range(TPB):
                        last = nc.vector.max(M8[:, t, :], L8[:, t, :])
                    last.then_inc(s_top, 1)
                    dve.wait_ge(s_top, 2 * b + 1)
                    settle(dve)
                    for t in range(TPB):
                        last = nc.vector.max_index(I8[:, t, :], M8[:, t, :], L8[:, t, :])
                    last.then_inc(s_top, 1)
                    dve.wait_ge(s_top, 2 * b + 2)
                    nc.vector.tensor_copy(M2[:, bass.ds(b * TPB, TPB), :], M8[:, :, 0:K]).then_inc(s_two, 1)
                    nc.vector.tensor_copy(I2[:, bass.ds(b * TPB, TPB), :], I8[:, :, 0:K]).then_inc(s_two, 1)
                if one:
                    add(s, 5)

            batch_steps(dve, step)

            done = [0]

            def then(ins):
                done[0] += 1
                ins.then_inc(s_r, 1)
                dve.wait_ge(s_r, done[0])

            col = lambda c, n: cst[:, c:c + n]
            dve.wait_ge(s_two, 2 * B)
            dve.wait_ge(s_wl, E * UNITS)
            dve.wait_ge(s_store, 32 * B)
            nc.vector.tensor_tensor(dl[:], M2[:, :, 1], M2[:, :, 0], ALU.subtract).then_inc(s_dl, 1)
            nc.vector.tensor_copy(tri[:], col(C_TRI, P))
            nc.vector.memset(ones[:], 1.0)
            nc.vector.memset(one8[:], 1.0)
            then(nc.vector.tensor_copy(idxf[:], I2[:].rearrange("p j k -> p k j")))
            for k in range(K):
                last = nc.vector.tensor_tensor(OH[:, k], col(C_E, E).unsqueeze(2).to_broadcast([P, E, NJ]),
                                               idxf[:, k].unsqueeze(1).to_broadcast([P, E, NJ]), ALU.is_equal)
            then(last)
            nc.vector.tensor_tensor(H[:], OH[:, 0], OH[:, 1], ALU.add).then_inc(s_H, 1)
            dve.wait_ge(s_rank, 1)
            flat = lambda t: t[:].rearrange("p e j -> p (e j)")
            then(nc.vector.tensor_copy(flat(CNT), pQ[:, 0:P]))
            then(nc.vector.tensor_tensor_scan(flat(INC), col(C_SEG, P), flat(CNT), 0.0, ALU.mult, ALU.add))
            then(nc.vector.tensor_scalar(ti[:], INC[:, :, NJ - 1], float(P - 1), None, ALU.add))
            then(nc.vector.tensor_scalar(ts[:], ti[:], 7, None, ALU.arith_shift_right))
            then(nc.vector.tensor_copy(nt[:], ts[:]))
            then(nc.vector.tensor_tensor_scan(tend[:], one8[:], nt[:], 0.0, ALU.mult, ALU.add))
            nc.vector.tensor_tensor(base[:], tend[:], nt[:], ALU.subtract)
            then(nc.vector.tensor_tensor(Z[:], INC[:], CNT[:], ALU.subtract))
            then(nc.vector.scalar_tensor_tensor(PO[:], base[:].unsqueeze(2).to_broadcast([P, E, NJ]), float(P), Z[:],
                                                ALU.mult, ALU.add))
            then(nc.vector.tensor_tensor(flat(Z), pK[:, 0:P], flat(PO), ALU.add))
            for k in range(K):
                last = nc.vector.tensor_tensor(PK[:, k], OH[:, k], Z[:], ALU.mult)
            then(last)
            then(nc.vector.reduce_sum(pos[:], PK[:].rearrange("p k e j -> p k j e"), axis=AX))
            posf = pos[:].rearrange("p k j -> p (k j)")
            then(nc.vector.tensor_copy(posi[:], posf))
            nc.vector.tensor_scalar(sli[:], posi[:], P - 1, None, ALU.bitwise_and)
            then(nc.vector.tensor_scalar(tli[:], posi[:], 7, None, ALU.arith_shift_right))
            nc.vector.tensor_copy(slf[:], sli[:])
            then(nc.vector.tensor_copy(tlf[:], tli[:]))
            q = KJ // 4
            for c in range(4):
                r = slice(c * q, (c + 1) * q)
                then(nc.vector.tensor_tensor(AT[:, r, 2, :], col(C_TILE, NT_SLOTS).unsqueeze(1).to_broadcast([P, q, NT_SLOTS]),
                                             tlf[:, r].unsqueeze(2).to_broadcast([P, q, NT_SLOTS]), ALU.is_equal))
                nc.vector.tensor_tensor(AT[:, r, 0, :], AT[:, r, 2, :],
                                        col(C_HI, KJ)[:, r].unsqueeze(2).to_broadcast([P, q, NT_SLOTS]), ALU.mult)
                nc.vector.tensor_scalar(AT[:, r, 1, :], AT[:, r, 2, :], col(C_P, 1), None, ALU.mult)
                nc.vector.tensor_tensor(BS[:, r, :], col(C_IOTA, P).unsqueeze(1).to_broadcast([P, q, P]),
                                        slf[:, r].unsqueeze(2).to_broadcast([P, q, P]), ALU.is_equal).then_inc(s_at, 1)
            then(nc.vector.tensor_tensor(ET[:], cst[0:1, C_TILE:C_TILE + NT_SLOTS].unsqueeze(2).to_broadcast([1, NT_SLOTS, E]),
                                         tend[0:1, :].unsqueeze(1).to_broadcast([1, NT_SLOTS, E]), ALU.is_ge))
            then(nc.vector.reduce_sum(ef[:], ET[:], axis=AX))
            then(nc.vector.tensor_scalar(eid[:], ef[:], float(E - 1), None, ALU.min))
            dve.wait_ge(s_e2, 1)
            then(nc.vector.tensor_scalar(den[:], e2[:], 1.0, None, ALU.add))
            then(nc.vector.reciprocal(wa[:], den[:]))
            then(nc.vector.tensor_tensor(wb[:], e2[:], wa[:], ALU.mult))
            nc.vector.tensor_scalar(gate[:, 0, :], wa[:], tg[:, 1:2], None, ALU.mult)
            nc.vector.tensor_scalar(gate[:, 1, :], wb[:], tg[:, 1:2], None, ALU.mult)
            dve.wait_ge(s_slots, 1)
            then(nc.vector.tensor_copy(SV[:].rearrange("p a i -> p (a i)"), pV[:, 0:3 * NT_SLOTS]))
            nc.vector.tensor_scalar(nh[:], SV[:, 2, :], -1.0, 1.0, ALU.mult, ALU.add)
            then(nc.vector.scalar_tensor_tensor(val[:], SV[:, 0, :], float(P), SV[:, 1, :], ALU.mult, ALU.add))
            then(nc.vector.tensor_scalar(gof[:], val[:], float(TOK), -float(TOK), ALU.is_ge, ALU.mult))
            then(nc.vector.tensor_tensor(gidx[:], gof[:], val[:], ALU.add))
            nc.vector.scalar_tensor_tensor(sidx[:], nh[:], col(C_PAD, 1), val[:], ALU.mult, ALU.add).then_inc(s_routed, 1)

            pX, pH3, pG, pY = bank[0], bank[2], bank[3], bank[4]

            def x_rest(i, p):
                dve.wait_ge(s_xh, i + 1)
                dve.wait_ge(s_xb, i + 1)
                nc.vector.tensor_tensor(xl[p][:], pX[:, 0:D], xh[p][:].bitcast(F32), ALU.subtract).then_inc(s_xl, 1)

            def g_rest(i):
                dve.wait_ge(s_gh, i + 1)
                nc.vector.tensor_tensor(gl[:], pG[:, :], gh[:].bitcast(F32), ALU.subtract).then_inc(s_gl, 1)

            def product(i):
                dve.wait_ge(s_silu, i + 1)
                dve.wait_ge(s_h3, i + 1)
                nc.vector.tensor_tensor(g[:], pH3[:, :], sl[:], ALU.mult).then_inc(s_g, 1)

            def result(i, p):
                dve.wait_ge(s_y, i + 1)
                if not isinstance(i, int) or i >= 2:
                    dve.wait_ge(s_scat[p], 16 * half(i, p))
                nc.vector.tensor_copy(ys[p][:], pY[:, 0:D]).then_inc(s_ys, 1)

            def tile(i, p, first, more):
                if more:
                    x_rest(i + 1, 1 - p)
                if not first:
                    g_rest(i - 1)
                product(i)
                if not first:
                    result(i - 1, 1 - p)

            x_rest(0, 0)
            tile(0, 0, True, True)
            tile(1, 1, False, True)
            tile(2, 0, False, True)
            with dve.Fori(1, (NT_SLOTS - 3) // 2) as r:
                for p in range(2):
                    tile(2 * r + 1 + p, 1 - p, False, True)
            tile(NT_SLOTS - 2, 1, False, True)
            tile(NT_SLOTS - 1, 0, False, False)
            g_rest(NT_SLOTS - 1)
            result(NT_SLOTS - 1, 0)

            dve.wait_ge(s_X2, 16)

            with dve.Fori(0, B // 2) as r:
                for p in range(2):
                    b = 2 * r + p
                    dve.wait_ge(s_yk[p], 16 * K * (r + 1))
                    for k in range(K):
                        for t in range(TPB):
                            xj = X2[:, bass.ds(b * TPB + t, 1), :].rearrange("p o d -> p (o d)")
                            last = nc.vector.scalar_tensor_tensor(xj, yk[p][k][:, t, :], gate[:, k, bass.ds(b * TPB + t, 1)],
                                                                  xj, ALU.mult, ALU.add)
                        last.then_inc(s_sum if k < K - 1 else s_fin, 1)
                        if k < K - 1:
                            dve.wait_ge(s_sum, b + 1)


def shape_tables():
    f = np.float32
    base = (np.arange(0, D, 2, dtype=f) + f(0.4 * D)) / f(1.4 * D)
    at = np.arange(S, dtype=f)
    scale = np.power(base[None, :], (at[:, None] / f(512.0))).astype(f)
    freqs = (f(1.0) / np.power(f(10000.0), np.arange(D // 2, dtype=f) / f(D // 2))).astype(f)
    angle = (at[:, None] * freqs[None, :]).astype(f)
    sin, cos = np.sin(angle).astype(f), np.cos(angle).astype(f)
    inv = f(1.0) / scale
    tabs = np.stack([cos * scale, sin * scale, cos * inv, sin * inv], 0)
    tabs = np.ascontiguousarray(tabs.transpose(2, 0, 1)).astype(f)
    u, v = np.arange(S, dtype=f)[None, :], np.arange(P, dtype=f)[:, None]
    first = np.where(u >= v, np.power(f(GAMMA), np.maximum(u - v, 0)), 0).astype(f)
    return tabs, np.ascontiguousarray(np.concatenate([first, first[:, 0:P]], 1))


def routing_constants():
    c = np.zeros((P, C_END), np.float32)
    p = np.arange(P)
    c[:, C_TRI:C_TRI + P] = p[:, None] < p[None, :]
    c[:, C_IOTA:C_IOTA + P] = p[None, :]
    c[:, C_SEG:C_SEG + P] = (p % NJ != 0)[None, :]
    c[:, C_HI:C_HI + KJ] = np.arange(KJ)[None, :]
    c[:, C_TILE:C_TILE + NT_SLOTS] = np.arange(NT_SLOTS)[None, :]
    c[:, C_E:C_E + E] = np.arange(E)[None, :]
    c[:, C_P] = p
    c[:, C_PAD] = K * TOK + p
    return c


def kernel(**inputs):
    import concourse.bacc as bacc
    from concourse.bass_utils import run_bass_kernel_spmd

    a = {k: np.asarray(v) for k, v in inputs.items()}
    order = np.concatenate([np.arange(0, D, 2), np.arange(1, D, 2)])
    chunks = lambda w: w.reshape(-1, P, w.shape[-1]).transpose(1, 0, 2).reshape(P, -1)

    qkv = np.stack([chunks(a["L0_xattn_Wq"].T[:, order]), chunks(a["L0_xattn_Wk"].T[:, order]),
                    chunks(a["L0_xattn_Wv"].T)], 1)
    f = lambda n: a["L0_ffn_" + n]
    w_all = np.stack([np.stack([chunks(f("W1")[e].T), chunks(f("W3")[e].T), chunks(f("W2")[e].T)]) for e in range(E)])
    w_all = w_all.reshape(E, KINDS, P, 2, UC).transpose(0, 1, 3, 2, 4).reshape(E, UNITS, P, UC)
    lora = np.stack([np.stack([np.concatenate([f("A1")[e], f("B1")[e].T], 1), np.concatenate([f("A3")[e], f("B3")[e].T], 1),
                               np.concatenate([f("A2")[e], f("B2")[e].T], 1)]) for e in range(E)])
    tabs, mask = shape_tables()
    arrays = {
        "x": a["x"].reshape(B, TPB, P, D).transpose(0, 2, 1, 3),
        "ctxT": a["ctx_1024"].transpose(0, 2, 1).reshape(B, CH, P, S).transpose(0, 2, 1, 3),
        "wqkv": qkv.reshape(P, 3, CH, D),
        "tables": tabs,
        "mask": mask,
        "gates_in": np.broadcast_to(np.concatenate([a["g_xattn"], a["g_ffn"]])[None, :], (P, 2)),
        "w_all": w_all,
        "lora": lora,
        "biases": np.concatenate([f("b1"), f("b3"), f("b2")], 1),
        "wgT": chunks(f("Wg").T).reshape(P, CH, E),
        "ident": np.eye(P, dtype=np.float32),
        "consts": routing_constants(),
    }
    arrays = {k + "_in": np.ascontiguousarray(v) for k, v in arrays.items()}
    nc = bacc.Bacc("TRN2", target_bir_lowering=False, num_devices=1)
    args = [nc.dram_tensor(k, v.shape, mybir.dt.from_np(v.dtype), kind="ExternalInput").ap() for k, v in arrays.items()]
    out = nc.dram_tensor("out", (B, S, D), F32, kind="ExternalOutput").ap()
    flamingo(nc, *args, out)
    result = run_bass_kernel_spmd(nc, [arrays], core_ids=[0])
    return result.results[0]["out"]
```

```python
from contextlib import ExitStack

import numpy as np

import concourse.bass as bass
from concourse import mybir

F32 = mybir.dt.float32
F32R = mybir.dt.float32r
BF16 = mybir.dt.bfloat16
I32 = mybir.dt.int32
U32 = mybir.dt.uint32
ALU = mybir.AluOpType
ACT = mybir.ActivationFunctionType
AX = mybir.AxisListType.X

P = 128
B, S, D = 8, 256, 256
E, HID, R, K = 8, 512, 16, 2
TOK = B * S
NJ = TOK // P
CH = D // P
HC = HID // P
TPB = S // P
NT_SLOTS = TOK * K // P + E - 1
XBUF = 4
KJ = K * NJ
EPS = 1e-5
GAMMA = 0.96875
KINDS = 3
WCOL = CH * HID
UNITS = 2 * KINDS
UC = WCOL // 2
LCOL = D + HID
LROWS = 3 * R
NSTAGE = 4
BROWS = 3 * 32
BCOL = 2 * HID + D

C_TRI, C_IOTA, C_SEG = 0, P, 2 * P
C_HI = 3 * P
C_TILE = C_HI + KJ
C_E = C_TILE + NT_SLOTS
C_P = C_E + E
C_PAD = C_P + 1
C_END = C_PAD + 1


def flamingo(nc, x, ctxT, wqkv, tables, mask, gates_in, w_all, lora, biases, wgT, ident_in, consts, out):
    xn2_d = nc.dram_tensor("xn2_rows", (TOK, D + K), F32, kind="Internal").ap()
    out_rows = out.rearrange("b s d -> (b s) d")
    lora_d = nc.dram_tensor("lora_parts", (E, LROWS, KINDS * LCOL), F32, kind="Internal").ap()

    whole = ExitStack()
    with whole:
        def sb(stack, name, shape, dt=F32):
            return stack.enter_context(nc.sbuf_tensor(name, shape, dt))

        def sem(name):
            return whole.enter_context(nc.semaphore(name))

        bank = [whole.enter_context(nc.psum_tensor(f"bank{i}", [P, 512], F32)) for i in range(8)]

        WH = sb(whole, "WH", [P, E * KINDS * WCOL], F32R)
        WL = sb(whole, "WL", [P, E * KINDS * WCOL], BF16)
        ident = sb(whole, "ident", [P, P])
        cst = sb(whole, "cst", [P, C_END])
        tg = sb(whole, "tg", [P, 2])
        M2 = sb(whole, "M2", [P, NJ, K])
        I2 = sb(whole, "I2", [P, NJ, K])

        early = ExitStack()
        tab = sb(early, "tab", [P, 4, S])
        msk = sb(early, "msk", [P, 2 * P])
        wq = sb(early, "wq", [P, 3, CH, D])
        wg = sb(early, "wg", [P, CH, E])
        gin = sb(early, "gin", [P, 2])
        xs = [sb(early, f"xs{p}", [P, TPB, D]) for p in range(2)]
        x2 = [sb(early, f"x2_{p}", [P, TPB, D]) for p in range(2)]
        cx = [sb(early, f"cx{p}", [P, CH, S]) for p in range(2)]
        xn = sb(early, "xn", [P, TPB, D])
        xnT = sb(early, "xnT", [P, CH, S])
        xn2 = [sb(early, f"xn2_{p}", [P, TPB, D]) for p in range(2)]
        xn2T = sb(early, "xn2T", [P, CH, S])
        qT = sb(early, "qT", [P, 2, S])
        kT = sb(early, "kT", [P, 2, S])
        v = [sb(early, f"v{p}", [P, TPB, D]) for p in range(2)]
        ret = sb(early, "ret", [P, 3 * P])
        tA = sb(early, "tA", [P, 2, S])
        tB = sb(early, "tB", [P, 2, S])
        stage = [sb(early, f"stage{i}", [P, UC]) for i in range(NSTAGE)]
        LS = [sb(early, f"LS{i}", [LROWS, LCOL], F32R) for i in range(2)]
        st1 = sb(early, "st1", [P, TPB, 6]); mv1 = sb(early, "mv1", [P, TPB, 2])
        eps_t = sb(early, "eps_t", [P, 1])
        sd1 = sb(early, "sd1", [P, TPB]); sd2 = sb(early, "sd2", [P, TPB])
        rs1 = sb(early, "rs1", [P, TPB]); nm1 = sb(early, "nm1", [P, TPB])
        st2 = sb(early, "st2", [P, TPB, 6]); mv2 = sb(early, "mv2", [P, TPB, 2])
        rs2 = sb(early, "rs2", [P, TPB]); nm2 = sb(early, "nm2", [P, TPB])
        L8 = sb(early, "L8", [P, TPB, E])
        M8 = sb(early, "M8", [P, TPB, 8])
        I8 = sb(early, "I8", [P, TPB, 8], U32)
        early.close()

        SEL = sb(whole, "SEL", [BROWS, E, P], BF16)
        B3 = sb(whole, "B3", [BROWS, BCOL], BF16)
        gate = sb(whole, "gate", [P, NJ, K])
        gidx = sb(whole, "gidx", [P, NT_SLOTS], U32)
        sidx = sb(whole, "sidx", [P, NT_SLOTS], U32)
        is1 = sb(whole, "is1", [P, NT_SLOTS]); is0 = sb(whole, "is0", [P, NT_SLOTS])
        eid = sb(whole, "eid", [1, NT_SLOTS], I32)
        route = ExitStack()
        braw = sb(route, "braw", [BROWS, BCOL]); bmid = sb(route, "bmid", [BROWS, BCOL], BF16)
        bhi = sb(route, "bhi", [BROWS, BCOL], BF16)
        tri = sb(route, "tri", [P, P], BF16); ones = sb(route, "ones", [P, P], BF16)
        idxf = sb(route, "idxf", [P, K, NJ])
        OH = sb(route, "OH", [P, K, E, NJ], BF16); H = sb(route, "H", [P, E, NJ], BF16)
        CNT = sb(route, "CNT", [P, E, NJ]); INC = sb(route, "INC", [P, E, NJ])
        ti = sb(route, "ti", [P, E], I32); ts = sb(route, "ts", [P, E], I32)
        nt = sb(route, "nt", [P, E]); tend = sb(route, "tend", [P, E]); base = sb(route, "base", [P, E])
        one8 = sb(route, "one8", [P, E])
        Z = sb(route, "Z", [P, E, NJ]); PO = sb(route, "PO", [P, E, NJ])
        PK = sb(route, "PK", [P, K, E, NJ]); pos = sb(route, "pos", [P, K, NJ])
        posi = sb(route, "posi", [P, KJ], I32); sli = sb(route, "sli", [P, KJ], I32)
        tli = sb(route, "tli", [P, KJ], I32)
        slf = sb(route, "slf", [P, KJ]); tlf = sb(route, "tlf", [P, KJ])
        AT = sb(route, "AT", [P, KJ, 3, NT_SLOTS], BF16)
        BS = sb(route, "BS", [P, KJ, P], BF16)
        SV = sb(route, "SV", [P, 3, NT_SLOTS]); val = sb(route, "val", [P, NT_SLOTS])
        gof = sb(route, "gof", [P, NT_SLOTS]); nh = sb(route, "nh", [P, NT_SLOTS])
        ET = sb(route, "ET", [1, NT_SLOTS, E]); ef = sb(route, "ef", [1, NT_SLOTS])
        dl = sb(route, "dl", [P, NJ]); e2 = sb(route, "e2", [P, NJ]); den = sb(route, "den", [P, NJ])
        wa = sb(route, "wa", [P, NJ]); wb = sb(route, "wb", [P, NJ])
        route.close()
        tiles = ExitStack()
        gi = [sb(tiles, f"gi{p}", [P, 1], U32) for p in range(2)]
        si = [sb(tiles, f"si{p}", [P, 1], U32) for p in range(2)]
        xg = [sb(tiles, f"xg{q}", [P, D + K]) for q in range(XBUF)]
        xh = [sb(tiles, f"xh{p}", [P, D], F32R) for p in range(2)]
        xl = [sb(tiles, f"xl{p}", [P, D], F32R) for p in range(2)]
        xb = [sb(tiles, f"xb{p}", [P, D], BF16) for p in range(2)]
        sl = sb(tiles, "sl", [P, HID]); g = sb(tiles, "g", [P, HID])
        gh = sb(tiles, "gh", [P, HID], F32R); gl = sb(tiles, "gl", [P, HID], F32R)
        gb = sb(tiles, "gb", [P, HID], BF16)
        ys = [sb(tiles, f"ys{p}", [P, D]) for p in range(2)]
        g0 = sb(tiles, "g0", [P, 1]); gs = [sb(tiles, f"gs{q}", [P, 1]) for q in range(XBUF)]
        tiles.close()

        s_waited = sem("s_waited")
        s_tab, s_gin, s_cst = sem("s_tab"), sem("s_gin"), sem("s_cst")
        s_xload, s_ctx = [sem(f"s_xload{p}") for p in range(2)], [sem(f"s_ctx{p}") for p in range(2)]
        s_stage = [sem(f"s_stage{i}") for i in range(NSTAGE)]
        s_lraw, s_lhi, s_lpart, s_lstore = sem("s_lraw"), sem("s_lhi"), sem("s_lpart"), sem("s_lstore")
        s_ls = [sem(f"s_ls{i}") for i in range(2)]
        s_store = [sem(f"s_store{p}") for p in range(2)]
        s_eps, s_tg = sem("s_eps"), sem("s_tg")
        s_unit, s_add, s_wh, s_wl = sem("s_unit"), sem("s_add"), sem("s_wh"), sem("s_wl")
        s_kproj, s_vproj, s_qproj = sem("s_kproj"), sem("s_vproj"), sem("s_qproj")
        s_krot, s_qrot, s_kT, s_qT, s_v = sem("s_krot"), sem("s_qrot"), sem("s_kT"), sem("s_qT"), sem("s_v")
        s_scores, s_ret, s_out, s_x2 = sem("s_scores"), sem("s_ret"), sem("s_out"), sem("s_x2")
        s_mv1, s_sd1, s_nm1, s_xn, s_xnTp, s_xnT = sem("s_mv1"), sem("s_sd1"), sem("s_nm1"), sem("s_xn"), sem("s_xnTp"), sem("s_xnT")
        s_mv2, s_sd2, s_nm2, s_xn2, s_xn2Tp, s_xn2T = (sem("s_mv2"), sem("s_sd2"), sem("s_nm2"), sem("s_xn2"), sem("s_xn2Tp"),
                                                 sem("s_xn2T"))
        s_logit, s_L = sem("s_logit"), sem("s_L")
        s_ln = sem("s_ln")
        s_top, s_two = sem("s_top"), sem("s_two")
        s_r = sem("s_r")
        s_braw, s_bzero, s_b = sem("s_braw"), sem("s_bzero"), sem("s_b")
        s_H, s_rank, s_at, s_slots = sem("s_H"), sem("s_rank"), sem("s_at"), sem("s_slots")
        s_routed, s_e2, s_dl = sem("s_routed"), sem("s_e2"), sem("s_dl")
        s_gates, s_gates_d, s_g0, s_gs = sem("s_gates"), sem("s_gates_d"), sem("s_g0"), sem("s_gs")
        s_gi, s_si = sem("s_gi"), sem("s_si")
        s_xg = [sem(f"s_xg{q}") for q in range(XBUF)]
        s_xT, s_xh, s_xl, s_xb = sem("s_xT"), sem("s_xh"), sem("s_xl"), sem("s_xb")
        s_h1, s_h3, s_silu, s_g = sem("s_h1"), sem("s_h3"), sem("s_silu"), sem("s_g")
        s_gT, s_gh, s_gl, s_gb = sem("s_gT"), sem("s_gh"), sem("s_gl"), sem("s_gb")
        s_y, s_ys = sem("s_y"), sem("s_ys")
        s_scat = [sem(f"s_scat{p}") for p in range(2)]

        block = whole.enter_context(nc.Block())

        pK, pQ, pV, pT, pS, pO = bank[:6]
        pW = bank[6:8]
        pL = pS[:, 3 * P:3 * P + TPB * E]

        def batch_steps(engine, step):
            for s in (0, 1):
                step(s, s % 2, True, s >= 1, False)
            with engine.Fori(1, B // 2) as r:
                for u in range(2):
                    step(2 * r + u, u, True, True, True)
            step(B, 0, False, True, True)
            step(B + 1, 1, False, False, True)

        def tile_steps(engine, step):
            turns = (NT_SLOTS - XBUF - (XBUF - 1)) // XBUF
            for i in range(XBUF):
                step(i, i, i == 0, True)
            with engine.Fori(1, turns + 1) as r:
                for q in range(XBUF):
                    step(XBUF * r + q, q, False, True)
            for i in range(XBUF * (turns + 1), NT_SLOTS):
                step(i, i % XBUF, False, i + 1 < NT_SLOTS)

        def half(s, u):
            return (s - u) // 2

        def pos_wait(eng, sm, val):
            if not isinstance(val, int) or val > 0:
                eng.wait_ge(sm, val)

        def settle(eng):
            eng.sem_inc(s_waited, 1)

        lspace = lambda e: WH[:, e * KINDS * WCOL:e * KINDS * WCOL + KINDS * LCOL]
        lraw = lspace(E - 1).bitcast(F32)
        lpart = [lspace(E - 2 - i) for i in range(3)]
        lA = [(k * LCOL, k * LCOL + (D if k < 2 else HID)) for k in range(KINDS)]
        lB = [(lA[k][1], (k + 1) * LCOL) for k in range(KINDS)]

        w_dst = lambda t, e, m: t[:, bass.ds((e * UNITS + m) * UC, UC)]

        @block.sync
        def _(sp):
            sp.sem_inc(s_store[0], 32)
            sp.sem_inc(s_store[1], 32)

            def load_x(t, u):
                pos_wait(sp, s_x2, t - 1)
                settle(sp)
                if not isinstance(t, int) or t >= 2:
                    sp.wait_ge(s_store[1 - u], 32 * ((t + u) // 2))
                    settle(sp)
                sp.dma_start(xs[u][:], x[t]).then_inc(s_xload[u], 16)

            def load_ctx(t, u):
                pos_wait(sp, s_vproj, t - 1)
                settle(sp)
                sp.dma_start(cx[u][:], ctxT[t]).then_inc(s_ctx[u], 16)

            def load_units(s, u, kind):
                i = s * KINDS + kind
                lb = (u * KINDS + kind) % 2
                pos_wait(sp, s_unit, 2 * i - 2)
                if isinstance(i, int) and i == 0:
                    sp.wait_ge(s_lstore, 48)
                settle(sp)
                sp.dma_start(LS[lb][:, :].bitcast(F32), lora_d[s, :, kind * LCOL:(kind + 1) * LCOL]).then_inc(s_ls[lb], 16)
                for m in (2 * kind, 2 * kind + 1):
                    pos_wait(sp, s_wl, s * UNITS + m - NSTAGE + 1)
                    settle(sp)
                    b = (u * UNITS + m) % NSTAGE
                    sp.dma_start(stage[b][:], w_all[s, m]).then_inc(s_stage[b], 16)

            sp.dma_start(gin[:], gates_in).then_inc(s_gin, 16)
            load_x(0, 0)
            sp.dma_start(cx[0][:], ctxT[0]).then_inc(s_ctx[0], 16)
            sp.dma_start(wq[:], wqkv).then_inc(s_tab, 16)
            sp.dma_start(ident[:], ident_in).then_inc(s_tab, 16)
            sp.dma_start(tab[:], tables).then_inc(s_tab, 16)
            sp.dma_start(msk[:], mask).then_inc(s_tab, 16)
            sp.dma_start(wg[:], wgT).then_inc(s_tab, 16)

            def turn(t, u):
                more = not isinstance(t, int) or t < B
                load_units(t - 1, 1 - u, 0)
                if more:
                    load_ctx(t, u)
                load_units(t - 1, 1 - u, 1)
                if more:
                    load_x(t, u)
                load_units(t - 1, 1 - u, 2)

            turn(1, 1)
            with sp.Fori(1, B // 2) as r:
                for u in range(2):
                    turn(2 * r + u, u)
            turn(B, 0)
            sp.dma_start(cst[:], consts).then_inc(s_cst, 16)
            for q in range(2):
                sp.wait_ge(s_store[q], 32 * (B // 2 + 1))
            sp.wait_ge(s_wl, E * UNITS)
            sp.wait_ge(s_L, B)
            sp.wait_ge(s_bzero, 1)
            for slot in range(3):
                sp.dma_start(braw[32 * slot:32 * slot + E, :], biases).then_inc(s_braw, 16)
            sp.wait_ge(s_gates, 1)
            sp.dma_start(xn2_d[:, D:D + K].rearrange("(j p) k -> p j k", p=P), gate[:]).then_inc(s_gates_d, 16)
            sp.wait_ge(s_gates_d, 16)
            sp.wait_ge(s_scat[0], 16 * ((NT_SLOTS + 1) // 2))
            sp.wait_ge(s_scat[1], 16 * (NT_SLOTS // 2))

        @block.tensor
        def _(pe):
            pe.wait_ge(s_tab, 5 * 16)

            def unit(s, u, m):
                kind, n = m // 2, s * UNITS + m
                i, lb = s * KINDS + kind, (u * KINDS + kind) % 2
                if m % 2 == 0:
                    pe.wait_ge(s_ls[lb], 16 * ((i - lb) // 2 + 1))
                pos_wait(pe, s_add, n - 1)
                L = LS[lb]
                if kind < 2:
                    c = m % 2
                    last = nc.tensor.matmul(pW[m % 2][:, :], L[:, c * P:(c + 1) * P], L[:, D:LCOL], start=True, stop=True)
                else:
                    for h in range(2):
                        c = 2 * (m % 2) + h
                        last = nc.tensor.matmul(pW[m % 2][:, h * D:(h + 1) * D], L[:, c * P:(c + 1) * P], L[:, HID:LCOL],
                                                start=True, stop=True)
                last.then_inc(s_unit, 1)

            def transposes(src, sig):
                for t in range(TPB):
                    for c in range(CH):
                        last = nc.tensor.transpose(pT[:, c * S + t * P:c * S + (t + 1) * P], src[:, t, c * P:(c + 1) * P],
                                                   ident[:])
                last.then_inc(sig, 1)

            def step(s, u, one, two, three):
                def units(*ms):
                    for m in ms:
                        unit(s, u, m)

                late = isinstance(s, int) and s == 0
                if one:
                    pe.wait_ge(s_ctx[u], 16 * (half(s, u) + 1))
                    pos_wait(pe, s_krot, s)
                    for m in range(2):
                        for c in range(CH):
                            last = nc.tensor.matmul(pK[:, m * S:(m + 1) * S], wq[:, 1, c, m * P:(m + 1) * P], cx[u][:, c, :],
                                                    start=(c == 0), stop=(c == CH - 1))
                    last.then_inc(s_kproj, 1)
                if three:
                    pe.wait_ge(s_xn2, s - 1)
                    transposes(xn2[u], s_xn2Tp)
                if two:
                    pe.wait_ge(s_kT, 2 * s)
                    pe.wait_ge(s_qT, 2 * s)
                    for kb in range(TPB):
                        o, n = kb * S, S - kb * P
                        for m in range(2):
                            last = nc.tensor.matmul(pS[:, o:o + n], kT[:, m, kb * P:(kb + 1) * P], qT[:, m, kb * P:S],
                                                    start=(m == 0), stop=(m == 1))
                    last.then_inc(s_scores, 1)
                if one:
                    if not late:
                        units(0, 1)
                    if three:
                        pe.wait_ge(s_xn2T, s - 1)
                    pe.wait_ge(s_xn, s + 1)
                    transposes(xn, s_xnTp)
                if two:
                    vv = v[1 - u]
                    pe.wait_ge(s_ret, s)
                    pe.wait_ge(s_v, s)
                    pos_wait(pe, s_x2, s - 1)
                    nc.tensor.matmul(pO[:, 0:D], ret[:, 0:P], vv[:, 0, :], start=True, stop=True)
                    nc.tensor.matmul(pO[:, D:2 * D], ret[:, P:2 * P], vv[:, 0, :], start=True, stop=False)
                    nc.tensor.matmul(pO[:, D:2 * D], ret[:, 2 * P:3 * P], vv[:, 1, :], start=False, stop=True
                                     ).then_inc(s_out, 1)
                if one:
                    if not late:
                        units(2)
                    pos_wait(pe, s_v, s)
                    for t in range(TPB):
                        for c in range(CH):
                            last = nc.tensor.matmul(pV[:, t * D:(t + 1) * D], cx[u][:, c, t * P:(t + 1) * P], wq[:, 2, c, :],
                                                    start=(c == 0), stop=(c == CH - 1))
                    last.then_inc(s_vproj, 1)
                if three:
                    pe.wait_ge(s_xn2T, s - 1)
                    if not one:
                        pe.wait_ge(s_L, s - 2)
                    for t in range(TPB):
                        for c in range(CH):
                            last = nc.tensor.matmul(pL[:, t * E:(t + 1) * E], xn2T[:, c, t * P:(t + 1) * P], wg[:, c, :],
                                                    start=(c == 0), stop=(c == CH - 1))
                    last.then_inc(s_logit, 1)
                if one:
                    if not late:
                        units(3)
                    pe.wait_ge(s_xnT, s + 1)
                    pos_wait(pe, s_qrot, s)
                    for m in range(2):
                        for c in range(CH):
                            last = nc.tensor.matmul(pQ[:, m * S:(m + 1) * S], wq[:, 0, c, m * P:(m + 1) * P], xnT[:, c, :],
                                                    start=(c == 0), stop=(c == CH - 1))
                    last.then_inc(s_qproj, 1)
                    units(*((0, 1, 2, 3) if late else ()), 4, 5)

            batch_steps(pe, step)

            Hf = H[:].rearrange("p e j -> p (e j)")
            pe.wait_ge(s_H, 1)
            nc.tensor.matmul(pK[:, 0:P], tri[:], Hf, start=True, stop=True)
            nc.tensor.matmul(pQ[:, 0:P], ones[:], Hf, start=True, stop=True).then_inc(s_rank, 1)
            for kj in range(KJ):
                if kj % (KJ // 4) == 0:
                    pe.wait_ge(s_at, kj // (KJ // 4) + 1)
                last = nc.tensor.matmul(pV[:, 0:3 * NT_SLOTS], BS[:, kj, :], AT[:, kj].rearrange("p a i -> p (a i)"),
                                        start=(kj == 0), stop=(kj == KJ - 1))
            last.then_inc(s_slots, 1)

            pX, pH1, pH3, pG, pY = bank[0], bank[1], bank[2], bank[3], bank[4]

            def x_transposes(i, q):
                pe.wait_ge(s_xg[q], 16 * ((i - q) // XBUF + 1))
                if not isinstance(i, int) or i > 0:
                    pe.wait_ge(s_xh, i)
                    pe.wait_ge(s_xb, i)
                    pe.wait_ge(s_xl, i)
                for c in range(CH):
                    last = nc.tensor.transpose(pX[:, c * P:(c + 1) * P], xg[q][:, c * P:(c + 1) * P], ident[:])
                last.then_inc(s_xT, 1)

            def up(dst, i, p, e, kind, sig):
                if kind == 0:
                    pos_wait(pe, s_silu, i)
                nc.tensor.matmul(dst[:, :], SEL[:].rearrange("p e q -> p (e q)")[:, bass.ds(e * P, P)],
                                 B3[:, kind * HID:(kind + 1) * HID], start=True, stop=False)
                for part, (lhs, W, ready) in enumerate(((xh, WH, s_xh), (xl, WH, s_xl), (xb, WL, s_xb))):
                    if kind == 0:
                        pe.wait_ge(ready, i + 1)
                    for c in range(CH):
                        last = nc.tensor.matmul(dst[:, :], lhs[p][:, c * P:(c + 1) * P],
                                                W[:, bass.ds(e * (UNITS * UC) + (2 * kind + c) * UC, HID)],
                                                start=False, stop=(part == 2 and c == CH - 1))
                last.then_inc(sig, 1)

            def g_transposes(i):
                pe.wait_ge(s_g, i + 1)
                for c in range(HC):
                    last = nc.tensor.transpose(pG[:, c * P:(c + 1) * P], g[:, c * P:(c + 1) * P], ident[:])
                last.then_inc(s_gT, 1)

            def down(i, e):
                pos_wait(pe, s_ys, i)
                nc.tensor.matmul(pY[:, 0:D], SEL[:].rearrange("p e q -> p (e q)")[:, bass.ds(e * P, P)], B3[:, 2 * HID:BCOL],
                                 start=True, stop=False)
                for part, (lhs, W, ready) in enumerate(((gh, WH, s_gh), (gl, WH, s_gl), (gb, WL, s_gb))):
                    pe.wait_ge(ready, i + 1)
                    for c in range(HC):
                        last = nc.tensor.matmul(pY[:, 0:D], lhs[:, c * P:(c + 1) * P],
                                                W[:, bass.ds(e * (UNITS * UC) + 4 * UC + c * D, D)],
                                                start=False, stop=(part == 2 and c == HC - 1))
                last.then_inc(s_y, 1)

            def expert(i):
                return pe.value_load(eid[0:1, bass.ds(i, 1)], min_val=0, max_val=E - 1)

            def tile(i, q, first, more):
                p = q % 2
                if more:
                    x_transposes(i + 1, (q + 1) % XBUF)
                e = expert(i)
                up(pH1, i, p, e, 0, s_h1)
                if not first:
                    g_transposes(i - 1)
                up(pH3, i, p, e, 1, s_h3)
                if not first:
                    down(i - 1, expert(i - 1))

            pe.wait_ge(s_routed, 1)
            pe.wait_ge(s_b, 1)
            x_transposes(0, 0)
            tile_steps(pe, tile)
            g_transposes(NT_SLOTS - 1)
            down(NT_SLOTS - 1, expert(NT_SLOTS - 1))

        @block.scalar
        def _(act):
            act.dma_start(lraw, lora).then_inc(s_lraw, 16)
            act.wait_ge(s_eps, 1)
            act.wait_ge(s_gin, 16)
            nc.scalar.activation(tg[:], gin[:], ACT.Tanh).then_inc(s_tg, 1)

            def rounded_factors():
                act.wait_ge(s_lraw, 16)
                nc.scalar.activation(lpart[0], lraw, ACT.Copy).then_inc(s_lhi, 1)
                for part, cols in ((1, lB), (2, lA)):
                    for a, b in cols:
                        last = nc.scalar.activation(lpart[part][:, a:b], lraw[:, a:b], ACT.Copy)
                    last.then_inc(s_lpart, 1)
                act.wait_ge(s_lpart, 2 + 2 * KINDS)
                for part in range(3):
                    act.dma_start(lora_d[:, part * R:(part + 1) * R, :], lpart[part].bitcast(F32)).then_inc(s_lstore, 16)

            def weight_hi(s, u, m):
                act.wait_ge(s_add, s * UNITS + m + 1)
                nc.scalar.activation(w_dst(WH, s, m), stage[(u * UNITS + m) % NSTAGE][:], ACT.Copy).then_inc(s_wh, 1)

            def normal(src, rs, nm, dst, sig):
                for t in range(TPB):
                    last = nc.scalar.activation(dst[:, t, :], src[:, t, :], ACT.Identity, scale=rs[:, t:t + 1],
                                                bias=nm[:, t:t + 1])
                last.then_inc(sig, 1)

            def step(s, u, one, two, three):
                if one:
                    act.wait_ge(s_mv1, s + 1)
                    nc.scalar.activation(sd1[:], mv1[:, :, 1], ACT.Sqrt, bias=eps_t[:]).then_inc(s_sd1, 1)
                    act.wait_ge(s_nm1, s + 1)
                    pos_wait(act, s_xnTp, s)
                    normal(xs[u], rs1, nm1, xn, s_xn)
                if isinstance(s, int) and s == 0:
                    rounded_factors()
                if three:
                    act.wait_ge(s_xn2Tp, s - 1)
                    nc.scalar.activation(xn2T[:].rearrange("p c t -> p (c t)"), pT[:, :], ACT.Copy).then_inc(s_xn2T, 1)
                late = isinstance(s, int) and s == 0
                if one:
                    if not late:
                        weight_hi(s, u, 0)
                        weight_hi(s, u, 1)
                    act.wait_ge(s_xnTp, s + 1)
                    nc.scalar.activation(xnT[:].rearrange("p c t -> p (c t)"), pT[:, :], ACT.Copy).then_inc(s_xnT, 1)
                    act.wait_ge(s_vproj, s + 1)
                    nc.scalar.activation(v[u][:].rearrange("p t d -> p (t d)"), pV[:, :], ACT.Copy).then_inc(s_v, 1)
                if two:
                    q = 1 - u
                    if not one:
                        act.wait_ge(s_store[q], 32 * (B // 2))
                    act.wait_ge(s_mv2, s)
                    nc.scalar.activation(sd2[:], mv2[:, :, 1], ACT.Sqrt, bias=eps_t[:]).then_inc(s_sd2, 1)
                    act.wait_ge(s_nm2, s)
                    normal(x2[q], rs2, nm2, xn2[q], s_xn2)
                if one:
                    for m in range(0 if late else 2, 4):
                        weight_hi(s, u, m)
                if two:
                    rows = bass.ds((s - 1) * S, S)
                    act.wait_ge(s_x2, s)
                    act.wait_ge(s_xn2, s)
                    settle(act)
                    for rows_d, buf in ((out_rows, x2[q]), (xn2_d, xn2[q])):
                        act.dma_start(rows_d[rows, 0:D].rearrange("(t p) d -> p t d", p=P), buf[:]).then_inc(s_store[q], 16)
                if one:
                    for m in range(4, UNITS):
                        weight_hi(s, u, m)

            batch_steps(act, step)
            act.wait_ge(s_dl, 1)
            nc.scalar.activation(e2[:], dl[:], ACT.Exp).then_inc(s_e2, 1)

            pX, pH1, pG = bank[0], bank[1], bank[3]

            def x_parts(i, p):
                act.wait_ge(s_xT, i + 1)
                pos_wait(act, s_h3, i - 1)
                nc.scalar.activation(xh[p][:], pX[:, 0:D], ACT.Copy).then_inc(s_xh, 1)
                nc.scalar.activation(xb[p][:], pX[:, 0:D], ACT.Copy).then_inc(s_xb, 1)

            def g_parts(i):
                act.wait_ge(s_gT, i + 1)
                pos_wait(act, s_y, i)
                nc.scalar.activation(gh[:], pG[:, :], ACT.Copy).then_inc(s_gh, 1)
                act.wait_ge(s_gh, i + 1)
                nc.scalar.activation(gb[:], gh[:].bitcast(F32), ACT.Copy).then_inc(s_gb, 1)

            def tile(i, q, first, more):
                p = q % 2
                if more:
                    x_parts(i + 1, 1 - p)
                if not first:
                    g_parts(i - 1)
                act.wait_ge(s_h1, i + 1)
                pos_wait(act, s_g, i)
                nc.scalar.activation(sl[:], pH1[:, :], ACT.Silu).then_inc(s_silu, 1)

            act.wait_ge(s_routed, 1)
            x_parts(0, 0)
            tile_steps(act, tile)
            g_parts(NT_SLOTS - 1)

        @block.gpsimd
        def _(pool):
            def weight_lo(s, u, m):
                pool.wait_ge(s_wh, s * UNITS + m + 1)
                nc.gpsimd.tensor_tensor(w_dst(WL, s, m), stage[(u * UNITS + m) % NSTAGE][:], w_dst(WH, s, m).bitcast(F32),
                                        ALU.subtract).then_inc(s_wl, 1)

            def rotated(dst, sig):
                nc.gpsimd.tensor_tensor(dst[:, 0, :], tA[:, 0, :], tB[:, 1, :], ALU.subtract).then_inc(sig, 1)
                nc.gpsimd.tensor_tensor(dst[:, 1, :], tA[:, 1, :], tB[:, 0, :], ALU.add).then_inc(sig, 1)

            nc.gpsimd.memset(eps_t[:], EPS).then_inc(s_eps, 1)
            pool.wait_ge(s_lhi, 1)
            for a, b in lB:
                nc.gpsimd.tensor_tensor(lpart[2][:, a:b], lraw[:, a:b], lpart[0][:, a:b].bitcast(F32), ALU.subtract
                                        ).then_inc(s_lpart, 1)

            def step(s, u, one, two, three):
                if one:
                    pool.wait_ge(s_krot, s + 1)
                    if two:
                        pool.wait_ge(s_scores, s)
                    rotated(kT, s_kT)
                    late = isinstance(s, int) and s == 0
                    if not late:
                        for m in range(4):
                            weight_lo(s, u, m)
                    pool.wait_ge(s_qrot, s + 1)
                    rotated(qT, s_qT)
                    for m in range(0 if late else 4, UNITS):
                        weight_lo(s, u, m)

            batch_steps(pool, step)

            pool.wait_ge(s_L, B)
            for q in range(2):
                pool.wait_ge(s_store[q], 32 * (B // 2 + 1))
            nc.gpsimd.memset(braw[:, :], 0.0).then_inc(s_bzero, 1)
            nc.gpsimd.memset(SEL[:], 0.0).then_inc(s_bzero, 1)
            pool.wait_ge(s_bzero, 2)
            for slot in range(3):
                part = SEL[32 * slot:32 * slot + E, :, :]
                nc.gpsimd.affine_select(out=part, in_=part, compare_op=ALU.not_equal, fill=1.0, base=0,
                                        pattern=[[-1, E], [0, P]], channel_multiplier=1).then_inc(s_bzero, 1)
            pool.wait_ge(s_bzero, 5)
            pool.wait_ge(s_braw, 48)
            nc.gpsimd.tensor_copy(bhi[:], braw[:]).then_inc(s_bzero, 1)
            nc.gpsimd.tensor_copy(B3[:], braw[:]).then_inc(s_bzero, 1)
            pool.wait_ge(s_bzero, 7)
            nc.gpsimd.tensor_tensor(braw[:], braw[:], bhi[:], ALU.subtract).then_inc(s_bzero, 1)
            pool.wait_ge(s_bzero, 8)
            nc.gpsimd.tensor_copy(bmid[:], braw[:]).then_inc(s_bzero, 1)
            pool.wait_ge(s_bzero, 9)
            nc.gpsimd.tensor_copy(B3[32:64, :], braw[32:64, :]).then_inc(s_bzero, 1)
            pool.wait_ge(s_bzero, 10)
            nc.gpsimd.tensor_tensor(B3[64:96, :], braw[64:96, :], bmid[64:96, :], ALU.subtract).then_inc(s_b, 1)
            pool.wait_ge(s_b, 1)

            def gather(i, q):
                pos_wait(pool, s_xT, i - XBUF + 1)
                pos_wait(pool, s_gs, i - XBUF + 1)
                p = q % 2
                if not isinstance(i, int) or i >= 2:
                    pool.wait_ge(s_xg[(q + 2) % XBUF], 16 * ((i - 2 - (q + 2) % XBUF) // XBUF + 1))
                nc.gpsimd.tensor_copy(gi[p][:], gidx[:, bass.ds(i, 1)]).then_inc(s_gi, 1)
                pool.wait_ge(s_gi, i + 1)
                settle(pool)
                nc.gpsimd.indirect_dma_start(out=xg[q][:], out_offset=None, in_=xn2_d,
                                             in_offset=bass.IndirectOffsetOnAxis(ap=gi[p][:, 0:1], axis=0)
                                             ).then_inc(s_xg[q], 16)

            def scatter(i, p):
                if not isinstance(i, int) or i >= 1:
                    pool.wait_ge(s_scat[1 - p], 16 * ((i + p) // 2))
                nc.gpsimd.tensor_copy(si[p][:], sidx[:, bass.ds(i, 1)]).then_inc(s_si, 1)
                pool.wait_ge(s_si, i + 1)
                pool.wait_ge(s_ys, i + 1)
                settle(pool)
                nc.gpsimd.indirect_dma_start(out=out_rows, out_offset=bass.IndirectOffsetOnAxis(ap=si[p][:, 0:1], axis=0),
                                             in_=ys[p][:], in_offset=None, bounds_check=TOK - 1,
                                             oob_is_err=False, compute_op=ALU.add).then_inc(s_scat[p], 16)

            pool.wait_ge(s_routed, 1)
            pool.wait_ge(s_gates_d, 16)
            for i in range(XBUF - 1):
                gather(i, i)

            def tile(i, q, first, more):
                if not isinstance(i, int) or i + XBUF - 1 < NT_SLOTS:
                    gather(i + (XBUF - 1), (q + XBUF - 1) % XBUF)
                if not first:
                    scatter(i - 1, (q + 1) % 2)

            tile_steps(pool, tile)
            scatter(NT_SLOTS - 1, (NT_SLOTS - 1) % 2)

        @block.vector
        def _(dve):
            def add(s, u, m):
                n, b = s * UNITS + m, (u * UNITS + m) % NSTAGE
                dve.wait_ge(s_unit, n + 1)
                dve.wait_ge(s_stage[b], 16 * ((n - b) // NSTAGE + 1))
                nc.vector.tensor_tensor(stage[b][:], pW[m % 2][:, :], stage[b][:], ALU.add).then_inc(s_add, 1)

            def rotate(bankt, which, sig):
                for dst, row in ((tA, 0), (tB, 1)):
                    t = tab[:, which + row, :].unsqueeze(1).to_broadcast([P, 2, S])
                    last = nc.vector.tensor_tensor(dst[:], bankt[:, :].rearrange("p (m t) -> p m t", m=2), t, ALU.mult)
                last.then_inc(sig, 1)

            def stats(src, st, mv, sig, n):
                for t in range(TPB):
                    last = nc.vector.bn_stats(st[:, t, :], src[:, t, :])
                last.then_inc(s_ln, 1)
                dve.wait_ge(s_ln, n + 1)
                settle(dve)
                for t in range(TPB):
                    last = nc.vector.bn_aggr(mv[:, t, :], st[:, t, :])
                last.then_inc(sig, 1)

            def scales(mv, sd, rs, nm, sig, n):
                nc.vector.reciprocal(rs[:], sd[:]).then_inc(s_ln, 1)
                dve.wait_ge(s_ln, n + 1)
                nc.vector.scalar_tensor_tensor(nm[:], mv[:, :, 0], -1.0, rs[:], ALU.mult, ALU.mult).then_inc(sig, 1)

            dve.wait_ge(s_xload[0], 16)
            stats(xs[0], st1, mv1, s_mv1, 0)
            dve.wait_ge(s_sd1, 1)
            scales(mv1, sd1, rs1, nm1, s_nm1, 1)
            dve.wait_ge(s_lhi, 1)
            for a, b in lA:
                nc.vector.tensor_tensor(lpart[1][:, a:b], lraw[:, a:b], lpart[0][:, a:b].bitcast(F32), ALU.subtract
                                        ).then_inc(s_lpart, 1)
            dve.wait_ge(s_tab, 5 * 16)
            dve.wait_ge(s_tg, 1)

            def step(s, u, one, two, three):
                first = isinstance(s, int) and s == 0
                ln = 4 * s - 2
                if one:
                    if not first:
                        dve.wait_ge(s_xload[u], 16 * (half(s, u) + 1))
                        dve.wait_ge(s_xn, s)
                        stats(xs[u], st1, mv1, s_mv1, ln)
                        dve.wait_ge(s_sd1, s + 1)
                        scales(mv1, sd1, rs1, nm1, s_nm1, ln + 1)
                        ln = ln + 2
                    dve.wait_ge(s_kproj, s + 1)
                    pos_wait(dve, s_qT, 2 * s)
                    rotate(pK, 2, s_krot)
                if two:
                    dve.wait_ge(s_scores, s)
                    pos_wait(dve, s_out, s - 1)
                    nc.vector.tensor_tensor(ret[:, 0:2 * P], pS[:, 0:2 * P], msk[:], ALU.mult)
                    nc.vector.tensor_tensor(ret[:, 2 * P:3 * P], pS[:, 2 * P:3 * P], msk[:, 0:P], ALU.mult).then_inc(s_ret, 1)
                if one and not first:
                    add(s, u, 0)
                    add(s, u, 1)
                if two:
                    q = 1 - u
                    if not one:
                        dve.wait_ge(s_store[q], 32 * (B // 2))
                    dve.wait_ge(s_out, s)
                    nc.vector.scalar_tensor_tensor(x2[q][:].rearrange("p t d -> p (t d)"), pO[:, :], tg[:, 0:1],
                                                   xs[q][:].rearrange("p t d -> p (t d)"), ALU.mult, ALU.add
                                                   ).then_inc(s_x2, 1)
                    dve.wait_ge(s_x2, s)
                    pos_wait(dve, s_xn2, s - 1)
                    stats(x2[q], st2, mv2, s_mv2, ln)
                if one and not first:
                    add(s, u, 2)
                if two:
                    dve.wait_ge(s_sd2, s)
                    scales(mv2, sd2, rs2, nm2, s_nm2, ln + 1)
                if three:
                    b = s - 2
                    dve.wait_ge(s_logit, b + 1)
                    nc.vector.tensor_copy(L8[:], pL[:, 0:TPB * E].rearrange("p (t e) -> p t e", t=TPB)).then_inc(s_L, 1)
                    dve.wait_ge(s_L, b + 1)
                    settle(dve)
                    for t in range(TPB):
                        last = nc.vector.max(M8[:, t, :], L8[:, t, :])
                    last.then_inc(s_top, 1)
                    dve.wait_ge(s_top, 2 * b + 1)
                    settle(dve)
                    for t in range(TPB):
                        last = nc.vector.max_index(I8[:, t, :], M8[:, t, :], L8[:, t, :])
                    last.then_inc(s_top, 1)
                    dve.wait_ge(s_top, 2 * b + 2)
                    nc.vector.tensor_copy(M2[:, bass.ds(b * TPB, TPB), :], M8[:, :, 0:K]).then_inc(s_two, 1)
                    nc.vector.tensor_copy(I2[:, bass.ds(b * TPB, TPB), :], I8[:, :, 0:K]).then_inc(s_two, 1)
                if one:
                    if not first:
                        add(s, u, 3)
                    dve.wait_ge(s_qproj, s + 1)
                    dve.wait_ge(s_kT, 2 * (s + 1))
                    rotate(pQ, 0, s_qrot)
                    for m in range(0 if first else 4, UNITS):
                        add(s, u, m)

            batch_steps(dve, step)

            done = [0]

            def then(ins):
                done[0] += 1
                ins.then_inc(s_r, 1)
                dve.wait_ge(s_r, done[0])

            col = lambda c, n: cst[:, c:c + n]
            dve.wait_ge(s_two, 2 * B)
            dve.wait_ge(s_wl, E * UNITS)
            for q in range(2):
                dve.wait_ge(s_store[q], 32 * (B // 2 + 1))
            dve.wait_ge(s_cst, 16)
            nc.vector.tensor_tensor(dl[:], M2[:, :, 1], M2[:, :, 0], ALU.subtract).then_inc(s_dl, 1)
            nc.vector.tensor_copy(tri[:], col(C_TRI, P))
            nc.vector.memset(ones[:], 1.0)
            nc.vector.memset(one8[:], 1.0)
            then(nc.vector.tensor_copy(idxf[:], I2[:].rearrange("p j k -> p k j")))
            for k in range(K):
                last = nc.vector.tensor_tensor(OH[:, k], col(C_E, E).unsqueeze(2).to_broadcast([P, E, NJ]),
                                               idxf[:, k].unsqueeze(1).to_broadcast([P, E, NJ]), ALU.is_equal)
            then(last)
            nc.vector.tensor_tensor(H[:], OH[:, 0], OH[:, 1], ALU.add).then_inc(s_H, 1)
            dve.wait_ge(s_rank, 1)
            flat = lambda t: t[:].rearrange("p e j -> p (e j)")
            then(nc.vector.tensor_copy(flat(CNT), pQ[:, 0:P]))
            then(nc.vector.tensor_tensor_scan(flat(INC), col(C_SEG, P), flat(CNT), 0.0, ALU.mult, ALU.add))
            then(nc.vector.tensor_scalar(ti[:], INC[:, :, NJ - 1], float(P - 1), None, ALU.add))
            then(nc.vector.tensor_scalar(ts[:], ti[:], 7, None, ALU.arith_shift_right))
            then(nc.vector.tensor_copy(nt[:], ts[:]))
            then(nc.vector.tensor_tensor_scan(tend[:], one8[:], nt[:], 0.0, ALU.mult, ALU.add))
            nc.vector.tensor_tensor(base[:], tend[:], nt[:], ALU.subtract)
            then(nc.vector.tensor_tensor(Z[:], INC[:], CNT[:], ALU.subtract))
            then(nc.vector.scalar_tensor_tensor(PO[:], base[:].unsqueeze(2).to_broadcast([P, E, NJ]), float(P), Z[:],
                                                ALU.mult, ALU.add))
            then(nc.vector.tensor_tensor(flat(Z), pK[:, 0:P], flat(PO), ALU.add))
            for k in range(K):
                last = nc.vector.tensor_tensor(PK[:, k], OH[:, k], Z[:], ALU.mult)
            then(last)
            then(nc.vector.reduce_sum(pos[:], PK[:].rearrange("p k e j -> p k j e"), axis=AX))
            posf = pos[:].rearrange("p k j -> p (k j)")
            then(nc.vector.tensor_copy(posi[:], posf))
            nc.vector.tensor_scalar(sli[:], posi[:], P - 1, None, ALU.bitwise_and)
            then(nc.vector.tensor_scalar(tli[:], posi[:], 7, None, ALU.arith_shift_right))
            nc.vector.tensor_copy(slf[:], sli[:])
            then(nc.vector.tensor_copy(tlf[:], tli[:]))
            q = KJ // 4
            for c in range(4):
                r = slice(c * q, (c + 1) * q)
                then(nc.vector.tensor_tensor(AT[:, r, 2, :], col(C_TILE, NT_SLOTS).unsqueeze(1).to_broadcast([P, q, NT_SLOTS]),
                                             tlf[:, r].unsqueeze(2).to_broadcast([P, q, NT_SLOTS]), ALU.is_equal))
                nc.vector.tensor_tensor(AT[:, r, 0, :], AT[:, r, 2, :],
                                        col(C_HI, KJ)[:, r].unsqueeze(2).to_broadcast([P, q, NT_SLOTS]), ALU.mult)
                nc.vector.tensor_scalar(AT[:, r, 1, :], AT[:, r, 2, :], col(C_P, 1), None, ALU.mult)
                nc.vector.tensor_tensor(BS[:, r, :], col(C_IOTA, P).unsqueeze(1).to_broadcast([P, q, P]),
                                        slf[:, r].unsqueeze(2).to_broadcast([P, q, P]), ALU.is_equal).then_inc(s_at, 1)
            then(nc.vector.tensor_tensor(ET[:], cst[0:1, C_TILE:C_TILE + NT_SLOTS].unsqueeze(2).to_broadcast([1, NT_SLOTS, E]),
                                         tend[0:1, :].unsqueeze(1).to_broadcast([1, NT_SLOTS, E]), ALU.is_ge))
            then(nc.vector.reduce_sum(ef[:], ET[:], axis=AX))
            then(nc.vector.tensor_scalar(eid[:], ef[:], float(E - 1), None, ALU.min))
            dve.wait_ge(s_e2, 1)
            then(nc.vector.tensor_scalar(den[:], e2[:], 1.0, None, ALU.add))
            then(nc.vector.reciprocal(wa[:], den[:]))
            then(nc.vector.tensor_tensor(wb[:], e2[:], wa[:], ALU.mult))
            nc.vector.tensor_scalar(gate[:, :, 0], wa[:], tg[:, 1:2], None, ALU.mult)
            nc.vector.tensor_scalar(gate[:, :, 1], wb[:], tg[:, 1:2], None, ALU.mult).then_inc(s_gates, 1)
            dve.wait_ge(s_slots, 1)
            then(nc.vector.tensor_copy(SV[:].rearrange("p a i -> p (a i)"), pV[:, 0:3 * NT_SLOTS]))
            nc.vector.tensor_scalar(nh[:], SV[:, 2, :], -1.0, 1.0, ALU.mult, ALU.add)
            then(nc.vector.scalar_tensor_tensor(val[:], SV[:, 0, :], float(P), SV[:, 1, :], ALU.mult, ALU.add))
            then(nc.vector.tensor_scalar(is1[:], val[:], float(TOK), None, ALU.is_ge))
            nc.vector.tensor_scalar(is0[:], is1[:], -1.0, 1.0, ALU.mult, ALU.add)
            then(nc.vector.scalar_tensor_tensor(gof[:], is1[:], -float(TOK), val[:], ALU.mult, ALU.add))
            nc.vector.tensor_copy(gidx[:], gof[:])
            nc.vector.scalar_tensor_tensor(sidx[:], nh[:], col(C_PAD, 1), gof[:], ALU.mult, ALU.add).then_inc(s_routed, 1)

            pX, pH3, pG, pY = bank[0], bank[2], bank[3], bank[4]

            def gates_of(i, q):
                dve.wait_ge(s_xg[q], 16 * ((i - q) // XBUF + 1))
                pos_wait(dve, s_gs, i)
                nc.vector.tensor_tensor(g0[:], xg[q][:, D:D + 1], is0[:, bass.ds(i, 1)], ALU.mult).then_inc(s_g0, 1)
                dve.wait_ge(s_g0, i + 1)
                nc.vector.scalar_tensor_tensor(gs[q][:], xg[q][:, D + 1:D + 2], is1[:, bass.ds(i, 1)], g0[:],
                                               ALU.mult, ALU.add).then_inc(s_gs, 1)

            def x_rest(i, p):
                dve.wait_ge(s_xh, i + 1)
                dve.wait_ge(s_xb, i + 1)
                nc.vector.tensor_tensor(xl[p][:], pX[:, 0:D], xh[p][:].bitcast(F32), ALU.subtract).then_inc(s_xl, 1)

            def g_rest(i):
                dve.wait_ge(s_gh, i + 1)
                nc.vector.tensor_tensor(gl[:], pG[:, :], gh[:].bitcast(F32), ALU.subtract).then_inc(s_gl, 1)

            def product(i):
                dve.wait_ge(s_silu, i + 1)
                dve.wait_ge(s_h3, i + 1)
                nc.vector.tensor_tensor(g[:], pH3[:, :], sl[:], ALU.mult).then_inc(s_g, 1)

            def result(i, q):
                p = q % 2
                dve.wait_ge(s_y, i + 1)
                if not isinstance(i, int) or i >= 2:
                    dve.wait_ge(s_scat[p], 16 * half(i, p))
                nc.vector.tensor_scalar(ys[p][:], pY[:, 0:D], gs[q][:], None, ALU.mult).then_inc(s_ys, 1)

            def tile(i, q, first, more):
                p = q % 2
                if more:
                    x_rest(i + 1, 1 - p)
                    gates_of(i + 1, (q + 1) % XBUF)
                if not first:
                    g_rest(i - 1)
                product(i)
                if not first:
                    result(i - 1, (q - 1) % XBUF)

            dve.wait_ge(s_routed, 1)
            x_rest(0, 0)
            gates_of(0, 0)
            tile_steps(dve, tile)
            g_rest(NT_SLOTS - 1)
            result(NT_SLOTS - 1, (NT_SLOTS - 1) % XBUF)


def shape_tables():
    f = np.float32
    base = (np.arange(0, D, 2, dtype=f) + f(0.4 * D)) / f(1.4 * D)
    at = np.arange(S, dtype=f)
    scale = np.power(base[None, :], (at[:, None] / f(512.0))).astype(f)
    freqs = (f(1.0) / np.power(f(10000.0), np.arange(D // 2, dtype=f) / f(D // 2))).astype(f)
    angle = (at[:, None] * freqs[None, :]).astype(f)
    sin, cos = np.sin(angle).astype(f), np.cos(angle).astype(f)
    inv = f(1.0) / scale
    tabs = np.stack([cos * scale, sin * scale, cos * inv, sin * inv], 0)
    tabs = np.ascontiguousarray(tabs.transpose(2, 0, 1)).astype(f)
    u, v = np.arange(S, dtype=f)[None, :], np.arange(P, dtype=f)[:, None]
    first = np.where(u >= v, np.power(f(GAMMA), np.maximum(u - v, 0)), 0).astype(f)
    return tabs, first


def routing_constants():
    c = np.zeros((P, C_END), np.float32)
    p = np.arange(P)
    c[:, C_TRI:C_TRI + P] = p[:, None] < p[None, :]
    c[:, C_IOTA:C_IOTA + P] = p[None, :]
    c[:, C_SEG:C_SEG + P] = (p % NJ != 0)[None, :]
    c[:, C_HI:C_HI + KJ] = np.arange(KJ)[None, :]
    c[:, C_TILE:C_TILE + NT_SLOTS] = np.arange(NT_SLOTS)[None, :]
    c[:, C_E:C_E + E] = np.arange(E)[None, :]
    c[:, C_P] = p
    c[:, C_PAD] = TOK + p
    return c


def kernel(**inputs):
    import concourse.bacc as bacc
    from concourse.bass_utils import run_bass_kernel_spmd

    a = {k: np.asarray(v) for k, v in inputs.items()}
    order = np.concatenate([np.arange(0, D, 2), np.arange(1, D, 2)])
    chunks = lambda w: w.reshape(-1, P, w.shape[-1]).transpose(1, 0, 2).reshape(P, -1)

    qkv = np.stack([chunks(a["L0_xattn_Wq"].T[:, order]), chunks(a["L0_xattn_Wk"].T[:, order]),
                    chunks(a["L0_xattn_Wv"].T)], 1)
    f = lambda n: a["L0_ffn_" + n]
    w_all = np.stack([np.stack([chunks(f("W1")[e].T), chunks(f("W3")[e].T), chunks(f("W2")[e].T)]) for e in range(E)])
    w_all = w_all.reshape(E, KINDS, P, 2, UC).transpose(0, 1, 3, 2, 4).reshape(E, UNITS, P, UC)
    lora = np.concatenate([np.concatenate([f("A1")[e], f("B1")[e].T, f("A3")[e], f("B3")[e].T, f("A2")[e], f("B2")[e].T], 1)
                           for e in range(E)])
    tabs, mask = shape_tables()
    arrays = {
        "x": a["x"].reshape(B, TPB, P, D).transpose(0, 2, 1, 3),
        "ctxT": a["ctx_1024"].transpose(0, 2, 1).reshape(B, CH, P, S).transpose(0, 2, 1, 3),
        "wqkv": qkv.reshape(P, 3, CH, D),
        "tables": tabs,
        "mask": mask,
        "gates_in": np.broadcast_to(np.concatenate([a["g_xattn"], a["g_ffn"]])[None, :], (P, 2)),
        "w_all": w_all,
        "lora": lora,
        "biases": np.concatenate([f("b1"), f("b3"), f("b2")], 1),
        "wgT": chunks(f("Wg").T).reshape(P, CH, E),
        "ident": np.eye(P, dtype=np.float32),
        "consts": routing_constants(),
    }
    arrays = {k + "_in": np.ascontiguousarray(v) for k, v in arrays.items()}
    nc = bacc.Bacc("TRN2", target_bir_lowering=False, num_devices=1)
    args = [nc.dram_tensor(k, v.shape, mybir.dt.from_np(v.dtype), kind="ExternalInput").ap() for k, v in arrays.items()]
    out = nc.dram_tensor("out", (B, S, D), F32, kind="ExternalOutput").ap()
    flamingo(nc, *args, out)
    result = run_bass_kernel_spmd(nc, [arrays], core_ids=[0])
    return result.results[0]["out"]
```

```python
from contextlib import ExitStack

import numpy as np

import concourse.bass as bass
from concourse import mybir

F32 = mybir.dt.float32
F32R = mybir.dt.float32r
BF16 = mybir.dt.bfloat16
I32 = mybir.dt.int32
U32 = mybir.dt.uint32
ALU = mybir.AluOpType
ACT = mybir.ActivationFunctionType
AX = mybir.AxisListType.X

P = 128
B, S, D = 8, 256, 256
E, HID, R, K = 8, 512, 16, 2
TOK = B * S
NJ = TOK // P
CH = D // P
HC = HID // P
TPB = S // P
NT_SLOTS = TOK * K // P + E - 1
XBUF = 4
KJ = K * NJ
EPS = 1e-5
GAMMA = 0.96875
KINDS = 3
WCOL = CH * HID
UNITS = 2 * KINDS
UC = WCOL // 2
LCOL = D + HID
LROWS = 3 * R
EARLY = 2
NSTAGE = 6
BCOL = 2 * HID + D

C_TRI, C_IOTA, C_SEG = 0, P, 2 * P
C_HI = 3 * P
C_TILE = C_HI + KJ
C_E = C_TILE + NT_SLOTS
C_P = C_E + E
C_PAD = C_P + 1
C_END = C_PAD + 1


def flamingo(nc, x, ctxT, wqkv, tables, mask, gates_in, w_all, lora, biases, wgT, ident_in, consts, out):
    xn2_d = nc.dram_tensor("xn2_rows", (TOK, D + K), F32, kind="Internal").ap()
    out_rows = out.rearrange("b s d -> (b s) d")
    lora_d = nc.dram_tensor("lora_parts", (E, LROWS, KINDS * LCOL), F32, kind="Internal").ap()

    whole = ExitStack()
    with whole:
        def sb(stack, name, shape, dt=F32):
            return stack.enter_context(nc.sbuf_tensor(name, shape, dt))

        def sem(name):
            return whole.enter_context(nc.semaphore(name))

        bank = [whole.enter_context(nc.psum_tensor(f"bank{i}", [P, 512], F32)) for i in range(8)]

        WH = sb(whole, "WH", [P, E * KINDS * WCOL], F32R)
        WL = sb(whole, "WL", [P, E * KINDS * WCOL], BF16)
        ident = sb(whole, "ident", [P, P])
        cst = sb(whole, "cst", [P, C_END])
        tg = sb(whole, "tg", [P, 2])
        M2 = sb(whole, "M2", [P, NJ, K])
        I2 = sb(whole, "I2", [P, NJ, K])

        early = ExitStack()
        tab = sb(early, "tab", [P, 4, S])
        msk = sb(early, "msk", [P, 2 * P])
        wq = sb(early, "wq", [P, 3, CH, D])
        wg = sb(early, "wg", [P, CH, E])
        gin = sb(early, "gin", [P, 2])
        xs = [sb(early, f"xs{p}", [P, TPB, D]) for p in range(2)]
        x2 = sb(early, "x2", [P, TPB, D])
        cx = [sb(early, f"cx{p}", [P, CH, S]) for p in range(2)]
        xn = sb(early, "xn", [P, TPB, D])
        xnT = sb(early, "xnT", [P, CH, S])
        xn2 = sb(early, "xn2", [P, TPB, D])
        xn2T = sb(early, "xn2T", [P, CH, S])
        qT = sb(early, "qT", [P, 2, S])
        kT = sb(early, "kT", [P, 2, S])
        v = [sb(early, f"v{p}", [P, TPB, D]) for p in range(2)]
        ret = sb(early, "ret", [P, 3 * P])
        tA = sb(early, "tA", [P, 2, S])
        tB = sb(early, "tB", [P, 2, S])
        stage = [sb(early, f"stage{i}", [P, UC]) for i in range(NSTAGE)]
        LS = [sb(early, f"LS{i}", [LROWS, LCOL], F32R) for i in range(2)]
        st1 = sb(early, "st1", [P, TPB, 6]); mv1 = sb(early, "mv1", [P, TPB, 2])
        eps_t = sb(early, "eps_t", [P, 1])
        sd1 = sb(early, "sd1", [P, TPB]); sd2 = sb(early, "sd2", [P, TPB])
        rs1 = sb(early, "rs1", [P, TPB]); nm1 = sb(early, "nm1", [P, TPB])
        st2 = sb(early, "st2", [P, TPB, 6]); mv2 = sb(early, "mv2", [P, TPB, 2])
        rs2 = sb(early, "rs2", [P, TPB]); nm2 = sb(early, "nm2", [P, TPB])
        L8 = sb(early, "L8", [P, TPB, E])
        M8 = sb(early, "M8", [P, TPB, 8])
        I8 = sb(early, "I8", [P, TPB, 8], U32)
        early.close()

        BB = sb(whole, "BB", [P, E, BCOL])
        gate = sb(whole, "gate", [P, NJ, K])
        gidx = sb(whole, "gidx", [P, NT_SLOTS], U32)
        sidx = sb(whole, "sidx", [P, NT_SLOTS], U32)
        is1 = sb(whole, "is1", [P, NT_SLOTS]); is0 = sb(whole, "is0", [P, NT_SLOTS])
        eid = sb(whole, "eid", [1, NT_SLOTS], I32)
        route = ExitStack()
        tri = sb(route, "tri", [P, P], BF16); ones = sb(route, "ones", [P, P], BF16)
        idxf = sb(route, "idxf", [P, K, NJ])
        OH = sb(route, "OH", [P, K, E, NJ], BF16); H = sb(route, "H", [P, E, NJ], BF16)
        CNT = sb(route, "CNT", [P, E, NJ]); INC = sb(route, "INC", [P, E, NJ])
        ti = sb(route, "ti", [P, E], I32); ts = sb(route, "ts", [P, E], I32)
        nt = sb(route, "nt", [P, E]); tend = sb(route, "tend", [P, E]); base = sb(route, "base", [P, E])
        one8 = sb(route, "one8", [P, E])
        Z = sb(route, "Z", [P, E, NJ]); PO = sb(route, "PO", [P, E, NJ])
        PK = sb(route, "PK", [P, K, E, NJ]); pos = sb(route, "pos", [P, K, NJ])
        posi = sb(route, "posi", [P, KJ], I32); sli = sb(route, "sli", [P, KJ], I32)
        tli = sb(route, "tli", [P, KJ], I32)
        slf = sb(route, "slf", [P, KJ]); tlf = sb(route, "tlf", [P, KJ])
        AT = sb(route, "AT", [P, KJ, 3, NT_SLOTS], BF16)
        BS = [sb(route, f"BS{i}", [P, KJ // 4, P], BF16) for i in range(2)]
        SV = sb(route, "SV", [P, 3, NT_SLOTS]); val = sb(route, "val", [P, NT_SLOTS])
        gof = sb(route, "gof", [P, NT_SLOTS]); nh = sb(route, "nh", [P, NT_SLOTS])
        ET = sb(route, "ET", [1, NT_SLOTS, E]); ef = sb(route, "ef", [1, NT_SLOTS])
        dl = sb(route, "dl", [P, NJ]); e2 = sb(route, "e2", [P, NJ]); den = sb(route, "den", [P, NJ])
        wa = sb(route, "wa", [P, NJ]); wb = sb(route, "wb", [P, NJ])
        route.close()
        tiles = ExitStack()
        gi = [sb(tiles, f"gi{p}", [P, 1], U32) for p in range(2)]
        si = [sb(tiles, f"si{p}", [P, 1], U32) for p in range(2)]
        xg = [sb(tiles, f"xg{q}", [P, D + K]) for q in range(XBUF)]
        xh = [sb(tiles, f"xh{p}", [P, D], F32R) for p in range(2)]
        xl = [sb(tiles, f"xl{p}", [P, D], F32R) for p in range(2)]
        xb = [sb(tiles, f"xb{p}", [P, D], BF16) for p in range(2)]
        h1 = sb(tiles, "h1", [P, HID])
        g = sb(tiles, "g", [P, HID])
        gh = sb(tiles, "gh", [P, HID], F32R); gl = sb(tiles, "gl", [P, HID], F32R)
        gb = sb(tiles, "gb", [P, HID], BF16)
        ys = [sb(tiles, f"ys{p}", [P, D]) for p in range(2)]
        gsel = sb(tiles, "gsel", [P, 1 + XBUF])
        g0, gs = gsel[:, XBUF:XBUF + 1], [gsel[:, q:q + 1] for q in range(XBUF)]
        tiles.close()

        s_waited = sem("s_waited")
        s_ktab, s_vtab, s_tab, s_gin, s_cst = sem("s_ktab"), sem("s_vtab"), sem("s_tab"), sem("s_gin"), sem("s_cst")
        s_xload, s_ctx = [sem(f"s_xload{p}") for p in range(2)], [sem(f"s_ctx{p}") for p in range(2)]
        s_stage = [sem(f"s_stage{i}") for i in range(NSTAGE)]
        s_lraw, s_lhi, s_lround = sem("s_lraw"), sem("s_lhi"), sem("s_lround")
        s_lstore = [sem(f"s_lstore{i}") for i in range(2)]
        s_lrest = [sem(f"s_lrest{i}") for i in (1, 2)]
        s_ls = [sem(f"s_ls{i}") for i in range(2)]
        s_store = sem("s_store")
        s_eps, s_tg = sem("s_eps"), sem("s_tg")
        s_unit, s_add, s_wh, s_wl = sem("s_unit"), sem("s_add"), sem("s_wh"), sem("s_wl")
        s_kproj, s_vproj, s_qproj = sem("s_kproj"), sem("s_vproj"), sem("s_qproj")
        s_krot, s_qrot, s_kT, s_qT, s_v = sem("s_krot"), sem("s_qrot"), sem("s_kT"), sem("s_qT"), sem("s_v")
        s_scores, s_ret, s_out, s_x2 = sem("s_scores"), sem("s_ret"), sem("s_out"), sem("s_x2")
        s_mv1, s_sd1, s_nm1, s_xn, s_xnTp, s_xnT = sem("s_mv1"), sem("s_sd1"), sem("s_nm1"), sem("s_xn"), sem("s_xnTp"), sem("s_xnT")
        s_mv2, s_sd2, s_nm2, s_xn2, s_xn2Tp, s_xn2T = (sem("s_mv2"), sem("s_sd2"), sem("s_nm2"), sem("s_xn2"), sem("s_xn2Tp"),
                                                 sem("s_xn2T"))
        s_logit, s_L = sem("s_logit"), sem("s_L")
        s_ln = sem("s_ln")
        s_top, s_two = sem("s_top"), sem("s_two")
        s_r = sem("s_r")
        s_bb = sem("s_bb")
        s_h1b, s_h3b, s_b2g = sem("s_h1b"), sem("s_h3b"), sem("s_b2g")
        s_H, s_rank, s_slots = sem("s_H"), sem("s_rank"), sem("s_slots")
        s_ind, s_bs, s_atj, s_atp = sem("s_ind"), sem("s_bs"), sem("s_atj"), sem("s_atp")
        s_routed, s_e2, s_dl = sem("s_routed"), sem("s_e2"), sem("s_dl")
        s_gates, s_gates_d, s_g0, s_gs = sem("s_gates"), sem("s_gates_d"), sem("s_g0"), sem("s_gs")
        s_gi, s_si = sem("s_gi"), sem("s_si")
        s_xg = [sem(f"s_xg{q}") for q in range(XBUF)]
        s_xT, s_xh, s_xl, s_xb = sem("s_xT"), sem("s_xh"), sem("s_xl"), sem("s_xb")
        s_h1, s_h3, s_silu, s_g = sem("s_h1"), sem("s_h3"), sem("s_silu"), sem("s_g")
        s_gT, s_gh, s_gl, s_gb = sem("s_gT"), sem("s_gh"), sem("s_gl"), sem("s_gb")
        s_y, s_ys = sem("s_y"), sem("s_ys")
        s_scat = [sem(f"s_scat{p}") for p in range(2)]

        block = whole.enter_context(nc.Block())

        pK, pQ, pV, pT, pS, pO = bank[:6]
        pW = bank[6:8]
        pL = pS[:, 3 * P:3 * P + TPB * E]

        def batch_steps(engine, step):
            for s in (0, 1):
                step(s, s % 2, True, s >= 1, False)
            with engine.Fori(1, B // 2) as r:
                for u in range(2):
                    step(2 * r + u, u, True, True, True)
            step(B, 0, False, True, True)
            step(B + 1, 1, False, False, True)

        def tile_steps(engine, step):
            turns = (NT_SLOTS - XBUF - (XBUF - 1)) // XBUF
            for i in range(XBUF):
                step(i, i, i == 0, True)
            with engine.Fori(1, turns + 1) as r:
                for q in range(XBUF):
                    step(XBUF * r + q, q, False, True)
            for i in range(XBUF * (turns + 1), NT_SLOTS):
                step(i, i % XBUF, False, i + 1 < NT_SLOTS)

        def half(s, u):
            return (s - u) // 2

        def pos_wait(eng, sm, val):
            if not isinstance(val, int) or val > 0:
                eng.wait_ge(sm, val)

        def settle(eng):
            eng.sem_inc(s_waited, 1)

        lspace = lambda e: WH[:, e * KINDS * WCOL:e * KINDS * WCOL + KINDS * LCOL]
        lraw = lspace(E - 1).bitcast(F32)
        lpart = [lspace(E - 2 - i) for i in range(3)]
        lA = [(k * LCOL, k * LCOL + (D if k < 2 else HID)) for k in range(KINDS)]
        lB = [(lA[k][1], (k + 1) * LCOL) for k in range(KINDS)]

        w_dst = lambda t, e, m: t[:, bass.ds((e * UNITS + m) * UC, UC)]

        @block.sync
        def _(sp):
            def load_x(t, u):
                pos_wait(sp, s_x2, t - 1)
                settle(sp)
                sp.dma_start(xs[u][:], x[t]).then_inc(s_xload[u], 16)

            def load_ctx(t, u):
                pos_wait(sp, s_vproj, t - 1)
                settle(sp)
                sp.dma_start(cx[u][:], ctxT[t]).then_inc(s_ctx[u], 16)

            def load_units(s, u, kind):
                i = s * KINDS + kind
                lb = (u * KINDS + kind) % 2
                pos_wait(sp, s_unit, 2 * i - 2)
                if kind == 0 and isinstance(s, int) and s in (0, EARLY):
                    sp.wait_ge(s_lstore[0 if s == 0 else 1], 48)
                settle(sp)
                sp.dma_start(LS[lb][:, :].bitcast(F32), lora_d[s, :, kind * LCOL:(kind + 1) * LCOL]).then_inc(s_ls[lb], 16)
                for m in (2 * kind, 2 * kind + 1):
                    pos_wait(sp, s_wl, s * UNITS + m - NSTAGE + 1)
                    settle(sp)
                    b = (u * UNITS + m) % NSTAGE
                    sp.dma_start(stage[b][:], w_all[s, m]).then_inc(s_stage[b], 16)

            load_x(0, 0)
            sp.dma_start(cx[0][:], ctxT[0]).then_inc(s_ctx[0], 16)
            sp.dma_start(wq[:, 1], wqkv[:, 1]).then_inc(s_ktab, 16)
            sp.dma_start(tab[:, 2:4], tables[:, 2:4]).then_inc(s_ktab, 16)
            sp.dma_start(ident[:], ident_in).then_inc(s_vtab, 16)
            sp.dma_start(wq[:, 2], wqkv[:, 2]).then_inc(s_vtab, 16)
            sp.dma_start(lraw, lora).then_inc(s_lraw, 16)
            sp.dma_start(wq[:, 0], wqkv[:, 0]).then_inc(s_tab, 16)
            sp.dma_start(tab[:, 0:2], tables[:, 0:2]).then_inc(s_tab, 16)
            sp.dma_start(msk[:], mask).then_inc(s_tab, 16)
            sp.dma_start(wg[:], wgT).then_inc(s_tab, 16)

            def turn(t, u, more=True, units=True):
                if units:
                    load_units(t - 2, u, 0)
                if more:
                    load_ctx(t, u)
                if units:
                    load_units(t - 2, u, 1)
                    load_units(t - 2, u, 2)
                if more:
                    load_x(t, u)

            turn(1, 1, units=False)
            turn(2, 0)
            turn(3, 1)
            turn(4, 0)
            turn(5, 1)
            with sp.Fori(3, B // 2) as r:
                for u in range(2):
                    turn(2 * r + u, u)
            turn(B, 0, more=False)
            turn(B + 1, 1, more=False)
            sp.dma_start(cst[:], consts).then_inc(s_cst, 16)
            sp.wait_ge(s_store, 32 * B)
            sp.wait_ge(s_wl, E * UNITS)
            sp.wait_ge(s_L, B)
            for e in range(E):
                sp.dma_start(BB[:, e, :], biases[e:e + 1, :].to_broadcast([P, BCOL])).then_inc(s_bb, 16)
                if e == 0:
                    sp.wait_ge(s_gates, 1)
                    sp.dma_start(xn2_d[:, D:D + K].rearrange("(j p) k -> p j k", p=P), gate[:]).then_inc(s_gates_d, 16)
            sp.wait_ge(s_gates_d, 16)
            sp.wait_ge(s_scat[0], 16 * ((NT_SLOTS + 1) // 2))
            sp.wait_ge(s_scat[1], 16 * (NT_SLOTS // 2))

        @block.tensor
        def _(pe):
            pe.wait_ge(s_ktab, 2 * 16)

            def unit(s, u, m):
                kind, n = m // 2, s * UNITS + m
                i, lb = s * KINDS + kind, (u * KINDS + kind) % 2
                if m % 2 == 0:
                    pe.wait_ge(s_ls[lb], 16 * ((i - lb) // 2 + 1))
                pos_wait(pe, s_add, n - 1)
                L = LS[lb]
                if kind < 2:
                    c = m % 2
                    last = nc.tensor.matmul(pW[m % 2][:, :], L[:, c * P:(c + 1) * P], L[:, D:LCOL], start=True, stop=True)
                else:
                    for h in range(2):
                        c = 2 * (m % 2) + h
                        last = nc.tensor.matmul(pW[m % 2][:, h * D:(h + 1) * D], L[:, c * P:(c + 1) * P], L[:, HID:LCOL],
                                                start=True, stop=True)
                last.then_inc(s_unit, 1)

            def transposes(src, sig):
                for t in range(TPB):
                    for c in range(CH):
                        last = nc.tensor.transpose(pT[:, c * S + t * P:c * S + (t + 1) * P], src[:, t, c * P:(c + 1) * P],
                                                   ident[:])
                last.then_inc(sig, 1)

            def step(s, u, one, two, three):
                def units(*ms):
                    if two:
                        for m in ms:
                            unit(s - 1, 1 - u, m)

                final = two and not one
                if one:
                    pe.wait_ge(s_ctx[u], 16 * (half(s, u) + 1))
                    pos_wait(pe, s_krot, s)
                    for m in range(2):
                        for c in range(CH):
                            last = nc.tensor.matmul(pK[:, m * S:(m + 1) * S], wq[:, 1, c, m * P:(m + 1) * P], cx[u][:, c, :],
                                                    start=(c == 0), stop=(c == CH - 1))
                    last.then_inc(s_kproj, 1)
                if three:
                    pe.wait_ge(s_xn2, s - 1)
                    transposes(xn2, s_xn2Tp)
                    if not two:
                        unit(E - 1, 1, 4)
                        unit(E - 1, 1, 5)
                if two:
                    pe.wait_ge(s_kT, 2 * s)
                    pe.wait_ge(s_qT, 2 * s)
                    for kb in range(TPB):
                        o, n = kb * S, S - kb * P
                        for m in range(2):
                            last = nc.tensor.matmul(pS[:, o:o + n], kT[:, m, kb * P:(kb + 1) * P], qT[:, m, kb * P:S],
                                                    start=(m == 0), stop=(m == 1))
                    last.then_inc(s_scores, 1)
                units(0, 1)
                if two:
                    vv = v[1 - u]
                    pe.wait_ge(s_ret, s)
                    pe.wait_ge(s_v, s)
                    pos_wait(pe, s_x2, s - 1)
                    nc.tensor.matmul(pO[:, 0:D], ret[:, 0:P], vv[:, 0, :], start=True, stop=True)
                    nc.tensor.matmul(pO[:, D:2 * D], ret[:, P:2 * P], vv[:, 0, :], start=True, stop=False)
                    nc.tensor.matmul(pO[:, D:2 * D], ret[:, 2 * P:3 * P], vv[:, 1, :], start=False, stop=True
                                     ).then_inc(s_out, 1)
                if one:
                    if not two:
                        pe.wait_ge(s_vtab, 2 * 16)
                    if three:
                        pe.wait_ge(s_xn2T, s - 1)
                    pe.wait_ge(s_xn, s + 1)
                    transposes(xn, s_xnTp)
                units(2, 3)
                if three:
                    pe.wait_ge(s_xn2T, s - 1)
                    if not one:
                        pe.wait_ge(s_L, s - 2)
                    for t in range(TPB):
                        for c in range(CH):
                            last = nc.tensor.matmul(pL[:, t * E:(t + 1) * E], xn2T[:, c, t * P:(t + 1) * P], wg[:, c, :],
                                                    start=(c == 0), stop=(c == CH - 1))
                    last.then_inc(s_logit, 1)
                if one:
                    pos_wait(pe, s_v, s)
                    for t in range(TPB):
                        for c in range(CH):
                            last = nc.tensor.matmul(pV[:, t * D:(t + 1) * D], cx[u][:, c, t * P:(t + 1) * P], wq[:, 2, c, :],
                                                    start=(c == 0), stop=(c == CH - 1))
                    last.then_inc(s_vproj, 1)
                if one:
                    if not two:
                        pe.wait_ge(s_tab, 4 * 16)
                    pe.wait_ge(s_xnT, s + 1)
                    pos_wait(pe, s_qrot, s)
                    for m in range(2):
                        for c in range(CH):
                            last = nc.tensor.matmul(pQ[:, m * S:(m + 1) * S], wq[:, 0, c, m * P:(m + 1) * P], xnT[:, c, :],
                                                    start=(c == 0), stop=(c == CH - 1))
                    last.then_inc(s_qproj, 1)
                if not final:
                    units(4, 5)

            batch_steps(pe, step)

            Hf = H[:].rearrange("p e j -> p (e j)")
            pe.wait_ge(s_H, 1)
            nc.tensor.matmul(pK[:, 0:P], tri[:], Hf, start=True, stop=True)
            nc.tensor.matmul(pQ[:, 0:P], ones[:], Hf, start=True, stop=True).then_inc(s_rank, 1)
            q = KJ // 4
            for kj in range(KJ):
                if kj % q == 0:
                    pe.wait_ge(s_bs, kj // q + 1)
                    pe.wait_ge(s_atj, kj // q + 1)
                    pe.wait_ge(s_atp, kj // q + 1)
                last = nc.tensor.matmul(pV[:, 0:3 * NT_SLOTS], BS[kj // q % 2][:, kj % q, :],
                                        AT[:, kj].rearrange("p a i -> p (a i)"), start=(kj == 0), stop=(kj == KJ - 1))
                if kj % q == q - 1:
                    last.then_inc(s_slots, 1)

            pX, pH1, pH3, pG, pY = bank[0], bank[1], bank[2], bank[3], bank[4]

            def x_transposes(i, q):
                pe.wait_ge(s_xg[q], 16 * ((i - q) // XBUF + 1))
                if not isinstance(i, int) or i > 0:
                    pe.wait_ge(s_xh, i)
                    pe.wait_ge(s_xb, i)
                    pe.wait_ge(s_xl, i)
                for c in range(CH):
                    last = nc.tensor.transpose(pX[:, c * P:(c + 1) * P], xg[q][:, c * P:(c + 1) * P], ident[:])
                last.then_inc(s_xT, 1)

            def up(dst, i, p, e, kind, sig):
                pos_wait(pe, s_h1b if kind == 0 else s_h3b, i)
                for part, (lhs, W, ready) in enumerate(((xh, WH, s_xh), (xl, WH, s_xl), (xb, WL, s_xb))):
                    if kind == 0:
                        pe.wait_ge(ready, i + 1)
                    for c in range(CH):
                        last = nc.tensor.matmul(dst[:, :], lhs[p][:, c * P:(c + 1) * P],
                                                W[:, bass.ds(e * (UNITS * UC) + (2 * kind + c) * UC, HID)],
                                                start=(part == 0 and c == 0), stop=(part == 2 and c == CH - 1))
                last.then_inc(sig, 1)

            def g_transposes(i):
                pe.wait_ge(s_g, i + 1)
                for c in range(HC):
                    last = nc.tensor.transpose(pG[:, c * P:(c + 1) * P], g[:, c * P:(c + 1) * P], ident[:])
                last.then_inc(s_gT, 1)

            def down(i, e):
                pos_wait(pe, s_ys, i)
                for part, (lhs, W, ready) in enumerate(((gh, WH, s_gh), (gl, WH, s_gl), (gb, WL, s_gb))):
                    pe.wait_ge(ready, i + 1)
                    for c in range(HC):
                        last = nc.tensor.matmul(pY[:, 0:D], lhs[:, c * P:(c + 1) * P],
                                                W[:, bass.ds(e * (UNITS * UC) + 4 * UC + c * D, D)],
                                                start=(part == 0 and c == 0), stop=(part == 2 and c == HC - 1))
                last.then_inc(s_y, 1)

            regs = [pe.alloc_register(f"expert{q}") for q in range(XBUF)]

            def expert(q):
                return pe.snap(regs[q], min_val=0, max_val=E - 1)

            def read_expert(i, q):
                pe.reg_load(regs[q], eid[0:1, bass.ds(i, 1)])

            def tile(i, q, first, more):
                p = q % 2
                if more and not first:
                    x_transposes(i + 1, (q + 1) % XBUF)
                e = expert(q)
                up(pH1, i, p, e, 0, s_h1)
                if first:
                    x_transposes(1, 1)
                if not first:
                    g_transposes(i - 1)
                up(pH3, i, p, e, 1, s_h3)
                if more:
                    read_expert(i + 1, (q + 1) % XBUF)
                if not first:
                    down(i - 1, expert((q - 1) % XBUF))

            pe.wait_ge(s_routed, 1)
            read_expert(0, 0)
            x_transposes(0, 0)
            tile_steps(pe, tile)
            g_transposes(NT_SLOTS - 1)
            down(NT_SLOTS - 1, expert((NT_SLOTS - 1) % XBUF))

        @block.scalar
        def _(act):
            act.dma_start(gin[:], gates_in).then_inc(s_gin, 16)
            act.wait_ge(s_gin, 16)
            nc.scalar.activation(tg[:], gin[:], ACT.Tanh).then_inc(s_tg, 1)
            act.wait_ge(s_eps, 1)

            def store_factors(part, e0, e1):
                act.dma_start(lora_d[e0:e1, part * R:(part + 1) * R, :], lpart[part][e0 * R:e1 * R, :].bitcast(F32)
                              ).then_inc(s_lstore[0 if e0 == 0 else 1], 16)

            def round_factors():
                act.wait_ge(s_lraw, 16)
                nc.scalar.activation(lpart[0], lraw, ACT.Copy).then_inc(s_lhi, 1)
                act.wait_ge(s_lhi, 1)
                store_factors(0, 0, EARLY)

            def pair_factors():
                for part, cols in ((1, lB), (2, lA)):
                    for a, b in cols:
                        last = nc.scalar.activation(lpart[part][:, a:b], lraw[:, a:b], ACT.Copy)
                    last.then_inc(s_lround, 1)
                for part in (1, 2):
                    act.wait_ge(s_lround, part)
                    act.wait_ge(s_lrest[part - 1], KINDS)
                    store_factors(part, 0, EARLY)

            def weight_hi(s, u, m):
                act.wait_ge(s_add, s * UNITS + m + 1)
                nc.scalar.activation(w_dst(WH, s, m), stage[(u * UNITS + m) % NSTAGE][:], ACT.Copy).then_inc(s_wh, 1)

            def normal(src, rs, nm, dst, sig):
                for t in range(TPB):
                    last = nc.scalar.activation(dst[:, t, :], src[:, t, :], ACT.Identity, scale=rs[:, t:t + 1],
                                                bias=nm[:, t:t + 1])
                last.then_inc(sig, 1)

            def step(s, u, one, two, three):
                if one:
                    act.wait_ge(s_mv1, s + 1)
                    nc.scalar.activation(sd1[:], mv1[:, :, 1], ACT.Sqrt, bias=eps_t[:]).then_inc(s_sd1, 1)
                    act.wait_ge(s_nm1, s + 1)
                    pos_wait(act, s_xnTp, s)
                    normal(xs[u], rs1, nm1, xn, s_xn)
                first = isinstance(s, int) and s == 0
                if first:
                    round_factors()
                if three:
                    act.wait_ge(s_xn2Tp, s - 1)
                    nc.scalar.activation(xn2T[:].rearrange("p c t -> p (c t)"), pT[:, :], ACT.Copy).then_inc(s_xn2T, 1)
                    if not two:
                        for m in range(4, UNITS):
                            weight_hi(E - 1, 1, m)
                if two:
                    weight_hi(s - 1, 1 - u, 0)
                    weight_hi(s - 1, 1 - u, 1)
                if one:
                    act.wait_ge(s_xnTp, s + 1)
                    nc.scalar.activation(xnT[:].rearrange("p c t -> p (c t)"), pT[:, :], ACT.Copy).then_inc(s_xnT, 1)
                if first:
                    pair_factors()
                if two:
                    if one:
                        weight_hi(s - 1, 1 - u, 2)
                    act.wait_ge(s_mv2, s)
                    nc.scalar.activation(sd2[:], mv2[:, :, 1], ACT.Sqrt, bias=eps_t[:]).then_inc(s_sd2, 1)
                if one:
                    act.wait_ge(s_vproj, s + 1)
                    nc.scalar.activation(v[u][:].rearrange("p t d -> p (t d)"), pV[:, :], ACT.Copy).then_inc(s_v, 1)
                if two:
                    act.wait_ge(s_nm2, s)
                    normal(x2, rs2, nm2, xn2, s_xn2)
                if two:
                    if not one:
                        weight_hi(s - 1, 1 - u, 2)
                    weight_hi(s - 1, 1 - u, 3)
                    rows = bass.ds((s - 1) * S, S)
                    act.wait_ge(s_x2, s)
                    act.wait_ge(s_xn2, s)
                    settle(act)
                    for rows_d, buf in ((out_rows, x2), (xn2_d, xn2)):
                        act.dma_start(rows_d[rows, 0:D].rearrange("(t p) d -> p t d", p=P), buf[:]).then_inc(s_store, 16)
                    for m in range(4, UNITS if one else 4):
                        weight_hi(s - 1, 1 - u, m)
                    if isinstance(s, int) and s == 1:
                        for part in range(3):
                            store_factors(part, EARLY, E)

            batch_steps(act, step)
            act.wait_ge(s_dl, 1)
            nc.scalar.activation(e2[:], dl[:], ACT.Exp).then_inc(s_e2, 1)
            q = KJ // 4
            for c in range(4):
                act.wait_ge(s_ind, c + 1)
                nc.scalar.activation(AT[:, c * q:(c + 1) * q, 1, :], AT[:, c * q:(c + 1) * q, 2, :], ACT.Copy,
                                     scale=cst[:, C_P:C_P + 1]).then_inc(s_atp, 1)

            pX, pH1, pG = bank[0], bank[1], bank[3]

            def x_parts(i, p):
                act.wait_ge(s_xT, i + 1)
                pos_wait(act, s_h3, i - 1)
                nc.scalar.activation(xh[p][:], pX[:, 0:D], ACT.Copy).then_inc(s_xh, 1)
                nc.scalar.activation(xb[p][:], pX[:, 0:D], ACT.Copy).then_inc(s_xb, 1)

            def g_parts(i):
                act.wait_ge(s_gT, i + 1)
                pos_wait(act, s_y, i)
                nc.scalar.activation(gh[:], pG[:, :], ACT.Copy).then_inc(s_gh, 1)
                act.wait_ge(s_gh, i + 1)
                nc.scalar.activation(gb[:], gh[:].bitcast(F32), ACT.Copy).then_inc(s_gb, 1)

            def tile(i, q, first, more):
                p = q % 2
                if more:
                    x_parts(i + 1, 1 - p)
                if not first:
                    g_parts(i - 1)
                act.wait_ge(s_h1b, i + 1)
                nc.scalar.activation(h1[:], h1[:], ACT.Silu).then_inc(s_silu, 1)
                e = act.value_load(eid[0:1, bass.ds(i, 1)], min_val=0, max_val=E - 1)
                act.wait_ge(s_gs, i + 1)
                if not isinstance(i, int) or i >= 2:
                    settle(act)
                    act.wait_ge(s_scat[p], 16 * half(i, p))
                nc.scalar.activation(ys[p][:], BB[:, bass.ds(e, 1), 2 * HID:BCOL].rearrange("p o d -> p (o d)"), ACT.Copy,
                                     scale=gs[q]).then_inc(s_b2g, 1)

            act.wait_ge(s_routed, 1)
            act.wait_ge(s_bb, 16 * E)
            x_parts(0, 0)
            tile_steps(act, tile)
            g_parts(NT_SLOTS - 1)

        @block.gpsimd
        def _(pool):
            def weight_lo(s, u, m):
                pool.wait_ge(s_wh, s * UNITS + m + 1)
                nc.gpsimd.tensor_tensor(w_dst(WL, s, m), stage[(u * UNITS + m) % NSTAGE][:], w_dst(WH, s, m).bitcast(F32),
                                        ALU.subtract).then_inc(s_wl, 1)

            def rotated(dst, sig):
                nc.gpsimd.tensor_tensor(dst[:, 0, :], tA[:, 0, :], tB[:, 1, :], ALU.subtract).then_inc(sig, 1)
                nc.gpsimd.tensor_tensor(dst[:, 1, :], tA[:, 1, :], tB[:, 0, :], ALU.add).then_inc(sig, 1)

            nc.gpsimd.memset(eps_t[:], EPS).then_inc(s_eps, 1)
            pool.wait_ge(s_lhi, 1)
            for a, b in lB[1:]:
                nc.gpsimd.tensor_tensor(lpart[2][:, a:b], lraw[:, a:b], lpart[0][:, a:b].bitcast(F32), ALU.subtract
                                        ).then_inc(s_lrest[1], 1)

            def step(s, u, one, two, three):
                if one:
                    pool.wait_ge(s_krot, s + 1)
                    if two:
                        pool.wait_ge(s_scores, s)
                    rotated(kT, s_kT)
                if two:
                    for m in range(4):
                        weight_lo(s - 1, 1 - u, m)
                if one:
                    pool.wait_ge(s_qrot, s + 1)
                    rotated(qT, s_qT)
                if two:
                    for m in range(4, UNITS):
                        weight_lo(s - 1, 1 - u, m)

            batch_steps(pool, step)

            pool.wait_ge(s_store, 32 * B)

            q = KJ // 4
            for c in range(4):
                pool.wait_ge(s_ind, c + 1)
                nc.gpsimd.tensor_tensor(AT[:, c * q:(c + 1) * q, 0, :], AT[:, c * q:(c + 1) * q, 2, :],
                                        cst[:, C_HI + c * q:C_HI + (c + 1) * q].unsqueeze(2).to_broadcast([P, q, NT_SLOTS]),
                                        ALU.mult).then_inc(s_atj, 1)

            def gather(i, q):
                pos_wait(pool, s_xT, i - XBUF + 1)
                pos_wait(pool, s_gs, i - XBUF + 1)
                p = q % 2
                if not isinstance(i, int) or i >= 2:
                    pool.wait_ge(s_xg[(q + 2) % XBUF], 16 * ((i - 2 - (q + 2) % XBUF) // XBUF + 1))
                nc.gpsimd.tensor_copy(gi[p][:], gidx[:, bass.ds(i, 1)]).then_inc(s_gi, 1)
                pool.wait_ge(s_gi, i + 1)
                settle(pool)
                nc.gpsimd.indirect_dma_start(out=xg[q][:], out_offset=None, in_=xn2_d,
                                             in_offset=bass.IndirectOffsetOnAxis(ap=gi[p][:, 0:1], axis=0)
                                             ).then_inc(s_xg[q], 16)

            def scatter(i, p):
                if not isinstance(i, int) or i >= 1:
                    pool.wait_ge(s_scat[1 - p], 16 * ((i + p) // 2))
                nc.gpsimd.tensor_copy(si[p][:], sidx[:, bass.ds(i, 1)]).then_inc(s_si, 1)
                pool.wait_ge(s_si, i + 1)
                pool.wait_ge(s_ys, i + 1)
                settle(pool)
                nc.gpsimd.indirect_dma_start(out=out_rows, out_offset=bass.IndirectOffsetOnAxis(ap=si[p][:, 0:1], axis=0),
                                             in_=ys[p][:], in_offset=None, bounds_check=TOK - 1,
                                             oob_is_err=False, compute_op=ALU.add).then_inc(s_scat[p], 16)

            pool.wait_ge(s_routed, 1)
            pool.wait_ge(s_gates_d, 16)
            for i in range(XBUF - 1):
                gather(i, i)

            def tile(i, q, first, more):
                if not isinstance(i, int) or i + XBUF - 1 < NT_SLOTS:
                    gather(i + (XBUF - 1), (q + XBUF - 1) % XBUF)
                if not first:
                    scatter(i - 1, (q + 1) % 2)

            tile_steps(pool, tile)
            scatter(NT_SLOTS - 1, (NT_SLOTS - 1) % 2)

        @block.vector
        def _(dve):
            def add(s, u, m):
                n, b = s * UNITS + m, (u * UNITS + m) % NSTAGE
                dve.wait_ge(s_unit, n + 1)
                dve.wait_ge(s_stage[b], 16 * ((n - b) // NSTAGE + 1))
                nc.vector.tensor_tensor(stage[b][:], pW[m % 2][:, :], stage[b][:], ALU.add).then_inc(s_add, 1)

            def rotate(bankt, which, row, sig=None):
                dst = (tA, tB)[row]
                t = tab[:, which + row, :].unsqueeze(1).to_broadcast([P, 2, S])
                last = nc.vector.tensor_tensor(dst[:], bankt[:, :].rearrange("p (m t) -> p m t", m=2), t, ALU.mult)
                if sig is not None:
                    last.then_inc(sig, 1)

            def sums(src, st):
                for t in range(TPB):
                    last = nc.vector.bn_stats(st[:, t, :], src[:, t, :])
                last.then_inc(s_ln, 1)

            def variance(st, mv, sig, n):
                dve.wait_ge(s_ln, n + 1)
                settle(dve)
                for t in range(TPB):
                    last = nc.vector.bn_aggr(mv[:, t, :], st[:, t, :])
                last.then_inc(sig, 1)

            def scale(sd, rs):
                nc.vector.reciprocal(rs[:], sd[:]).then_inc(s_ln, 1)

            def shift(mv, rs, nm, sig, n):
                dve.wait_ge(s_ln, n + 2)
                nc.vector.scalar_tensor_tensor(nm[:], mv[:, :, 0], -1.0, rs[:], ALU.mult, ALU.mult).then_inc(sig, 1)

            dve.wait_ge(s_xload[0], 16)
            sums(xs[0], st1)
            variance(st1, mv1, s_mv1, 0)
            dve.wait_ge(s_sd1, 1)
            scale(sd1, rs1)
            shift(mv1, rs1, nm1, s_nm1, 0)
            dve.wait_ge(s_ktab, 2 * 16)

            def factor_rests():
                dve.wait_ge(s_lhi, 1)
                for part, a, b in [(1, a, b) for a, b in lA] + [(2, *lB[0])]:
                    nc.vector.tensor_tensor(lpart[part][:, a:b], lraw[:, a:b], lpart[0][:, a:b].bitcast(F32), ALU.subtract
                                            ).then_inc(s_lrest[part - 1], 1)

            def step(s, u, one, two, three):
                first = isinstance(s, int) and s == 0
                ln = 4 * s - 2
                b = s - 2
                weight = lambda m: add(s - 1, 1 - u, m)
                if one:
                    if not first:
                        dve.wait_ge(s_xload[u], 16 * (half(s, u) + 1))
                        sums(xs[u], st1)
                    dve.wait_ge(s_kproj, s + 1)
                    pos_wait(dve, s_qT, 2 * s)
                    rotate(pK, 2, 0)
                    if not first:
                        variance(st1, mv1, s_mv1, ln)
                    rotate(pK, 2, 1, s_krot)
                    if first:
                        factor_rests()
                    if not first:
                        dve.wait_ge(s_sd1, s + 1)
                        dve.wait_ge(s_xn, s)
                        scale(sd1, rs1)
                        shift(mv1, rs1, nm1, s_nm1, ln)
                        ln = ln + 2
                if two:
                    dve.wait_ge(s_scores, s)
                    pos_wait(dve, s_out, s - 1)
                    nc.vector.tensor_tensor(ret[:, 0:2 * P], pS[:, 0:2 * P], msk[:], ALU.mult)
                    nc.vector.tensor_tensor(ret[:, 2 * P:3 * P], pS[:, 2 * P:3 * P], msk[:, 0:P], ALU.mult).then_inc(s_ret, 1)
                    weight(0)
                    weight(1)
                    if isinstance(s, int) and s == 1:
                        dve.wait_ge(s_tg, 1)
                    pos_wait(dve, s_store, 32 * (s - 1))
                    dve.wait_ge(s_out, s)
                    nc.vector.scalar_tensor_tensor(x2[:].rearrange("p t d -> p (t d)"), pO[:, :], tg[:, 0:1],
                                                   xs[1 - u][:].rearrange("p t d -> p (t d)"), ALU.mult, ALU.add
                                                   ).then_inc(s_x2, 1)
                    dve.wait_ge(s_x2, s)
                    sums(x2, st2)
                    if one:
                        weight(2)
                    variance(st2, mv2, s_mv2, ln)
                if three:
                    dve.wait_ge(s_logit, b + 1)
                    nc.vector.tensor_copy(L8[:], pL[:, 0:TPB * E].rearrange("p (t e) -> p t e", t=TPB)).then_inc(s_L, 1)
                if two:
                    dve.wait_ge(s_sd2, s)
                    pos_wait(dve, s_xn2, s - 1)
                    scale(sd2, rs2)
                if three:
                    dve.wait_ge(s_L, b + 1)
                    settle(dve)
                    for t in range(TPB):
                        last = nc.vector.max(M8[:, t, :], L8[:, t, :])
                    last.then_inc(s_top, 1)
                if two:
                    shift(mv2, rs2, nm2, s_nm2, ln)
                    if not one:
                        weight(2)
                    weight(3)
                if three:
                    dve.wait_ge(s_top, 2 * b + 1)
                    settle(dve)
                    for t in range(TPB):
                        last = nc.vector.max_index(I8[:, t, :], M8[:, t, :], L8[:, t, :])
                    last.then_inc(s_top, 1)
                if three:
                    dve.wait_ge(s_top, 2 * b + 2)
                    nc.vector.tensor_copy(M2[:, bass.ds(b * TPB, TPB), :], M8[:, :, 0:K]).then_inc(s_two, 1)
                    nc.vector.tensor_copy(I2[:, bass.ds(b * TPB, TPB), :], I8[:, :, 0:K]).then_inc(s_two, 1)
                if one:
                    if first:
                        dve.wait_ge(s_tab, 4 * 16)
                    dve.wait_ge(s_qproj, s + 1)
                    dve.wait_ge(s_kT, 2 * (s + 1))
                    rotate(pQ, 0, 0)
                    rotate(pQ, 0, 1, s_qrot)
                if two:
                    weight(4)
                if two:
                    weight(5)

            batch_steps(dve, step)

            done = [0]

            def then(ins):
                done[0] += 1
                ins.then_inc(s_r, 1)
                dve.wait_ge(s_r, done[0])

            col = lambda c, n: cst[:, c:c + n]
            dve.wait_ge(s_two, 2 * B)
            dve.wait_ge(s_wl, E * UNITS)
            dve.wait_ge(s_store, 32 * B)
            dve.wait_ge(s_cst, 16)
            nc.vector.tensor_tensor(dl[:], M2[:, :, 1], M2[:, :, 0], ALU.subtract).then_inc(s_dl, 1)
            nc.vector.tensor_copy(tri[:], col(C_TRI, P))
            nc.vector.memset(ones[:], 1.0)
            nc.vector.memset(one8[:], 1.0)
            then(nc.vector.tensor_copy(idxf[:], I2[:].rearrange("p j k -> p k j")))
            for k in range(K):
                last = nc.vector.tensor_tensor(OH[:, k], col(C_E, E).unsqueeze(2).to_broadcast([P, E, NJ]),
                                               idxf[:, k].unsqueeze(1).to_broadcast([P, E, NJ]), ALU.is_equal)
            then(last)
            nc.vector.tensor_tensor(H[:], OH[:, 0], OH[:, 1], ALU.add).then_inc(s_H, 1)
            dve.wait_ge(s_e2, 1)
            then(nc.vector.tensor_scalar(den[:], e2[:], 1.0, None, ALU.add))
            then(nc.vector.reciprocal(wa[:], den[:]))
            then(nc.vector.tensor_tensor(wb[:], e2[:], wa[:], ALU.mult))
            nc.vector.tensor_scalar(gate[:, :, 0], wa[:], tg[:, 1:2], None, ALU.mult)
            nc.vector.tensor_scalar(gate[:, :, 1], wb[:], tg[:, 1:2], None, ALU.mult).then_inc(s_gates, 1)
            dve.wait_ge(s_rank, 1)
            flat = lambda t: t[:].rearrange("p e j -> p (e j)")
            then(nc.vector.tensor_copy(flat(CNT), pQ[:, 0:P]))
            then(nc.vector.tensor_tensor_scan(flat(INC), col(C_SEG, P), flat(CNT), 0.0, ALU.mult, ALU.add))
            then(nc.vector.tensor_scalar(ti[:], INC[:, :, NJ - 1], float(P - 1), None, ALU.add))
            then(nc.vector.tensor_scalar(ts[:], ti[:], 7, None, ALU.arith_shift_right))
            then(nc.vector.tensor_copy(nt[:], ts[:]))
            then(nc.vector.tensor_tensor_scan(tend[:], one8[:], nt[:], 0.0, ALU.mult, ALU.add))
            nc.vector.tensor_tensor(base[:], tend[:], nt[:], ALU.subtract)
            then(nc.vector.tensor_tensor(Z[:], INC[:], CNT[:], ALU.subtract))
            then(nc.vector.scalar_tensor_tensor(PO[:], base[:].unsqueeze(2).to_broadcast([P, E, NJ]), float(P), Z[:],
                                                ALU.mult, ALU.add))
            then(nc.vector.tensor_tensor(flat(Z), pK[:, 0:P], flat(PO), ALU.add))
            for k in range(K):
                last = nc.vector.tensor_tensor(PK[:, k], OH[:, k], Z[:], ALU.mult)
            then(last)
            then(nc.vector.reduce_sum(pos[:], PK[:].rearrange("p k e j -> p k j e"), axis=AX))
            posf = pos[:].rearrange("p k j -> p (k j)")
            then(nc.vector.tensor_copy(posi[:], posf))
            nc.vector.tensor_scalar(sli[:], posi[:], P - 1, None, ALU.bitwise_and)
            then(nc.vector.tensor_scalar(tli[:], posi[:], 7, None, ALU.arith_shift_right))
            nc.vector.tensor_copy(slf[:], sli[:])
            then(nc.vector.tensor_copy(tlf[:], tli[:]))
            q = KJ // 4
            for c in range(4):
                r = slice(c * q, (c + 1) * q)
                nc.vector.tensor_tensor(AT[:, r, 2, :], col(C_TILE, NT_SLOTS).unsqueeze(1).to_broadcast([P, q, NT_SLOTS]),
                                        tlf[:, r].unsqueeze(2).to_broadcast([P, q, NT_SLOTS]), ALU.is_equal).then_inc(s_ind, 1)
                if c >= 2:
                    dve.wait_ge(s_slots, c - 1)
                nc.vector.tensor_tensor(BS[c % 2][:], col(C_IOTA, P).unsqueeze(1).to_broadcast([P, q, P]),
                                        slf[:, r].unsqueeze(2).to_broadcast([P, q, P]), ALU.is_equal).then_inc(s_bs, 1)
            then(nc.vector.tensor_tensor(ET[:], cst[0:1, C_TILE:C_TILE + NT_SLOTS].unsqueeze(2).to_broadcast([1, NT_SLOTS, E]),
                                         tend[0:1, :].unsqueeze(1).to_broadcast([1, NT_SLOTS, E]), ALU.is_ge))
            then(nc.vector.reduce_sum(ef[:], ET[:], axis=AX))
            then(nc.vector.tensor_scalar(eid[:], ef[:], float(E - 1), None, ALU.min))
            dve.wait_ge(s_slots, 4)
            then(nc.vector.tensor_copy(SV[:].rearrange("p a i -> p (a i)"), pV[:, 0:3 * NT_SLOTS]))
            nc.vector.tensor_scalar(nh[:], SV[:, 2, :], -1.0, 1.0, ALU.mult, ALU.add)
            then(nc.vector.scalar_tensor_tensor(val[:], SV[:, 0, :], float(P), SV[:, 1, :], ALU.mult, ALU.add))
            then(nc.vector.tensor_scalar(is1[:], val[:], float(TOK), None, ALU.is_ge))
            nc.vector.tensor_scalar(is0[:], is1[:], -1.0, 1.0, ALU.mult, ALU.add)
            then(nc.vector.scalar_tensor_tensor(gof[:], is1[:], -float(TOK), val[:], ALU.mult, ALU.add))
            nc.vector.tensor_copy(gidx[:], gof[:])
            nc.vector.scalar_tensor_tensor(sidx[:], nh[:], col(C_PAD, 1), gof[:], ALU.mult, ALU.add).then_inc(s_routed, 1)

            pX, pH1, pH3, pG, pY = bank[0], bank[1], bank[2], bank[3], bank[4]

            def gates_of(i, q):
                dve.wait_ge(s_xg[q], 16 * ((i - q) // XBUF + 1))
                pos_wait(dve, s_gs, i)
                nc.vector.tensor_tensor(g0, xg[q][:, D:D + 1], is0[:, bass.ds(i, 1)], ALU.mult).then_inc(s_g0, 1)
                dve.wait_ge(s_g0, i + 1)
                nc.vector.scalar_tensor_tensor(gs[q], xg[q][:, D + 1:D + 2], is1[:, bass.ds(i, 1)], g0,
                                               ALU.mult, ALU.add).then_inc(s_gs, 1)

            def x_rest(i, p):
                dve.wait_ge(s_xh, i + 1)
                dve.wait_ge(s_xb, i + 1)
                nc.vector.tensor_tensor(xl[p][:], pX[:, 0:D], xh[p][:].bitcast(F32), ALU.subtract).then_inc(s_xl, 1)

            def g_rest(i):
                dve.wait_ge(s_gh, i + 1)
                nc.vector.tensor_tensor(gl[:], pG[:, :], gh[:].bitcast(F32), ALU.subtract).then_inc(s_gl, 1)

            def biased(dst, src, i, e, kind, ready, sig):
                dve.wait_ge(ready, i + 1)
                b = BB[:, bass.ds(e, 1), kind * HID:(kind + 1) * HID].rearrange("p o h -> p (o h)")
                nc.vector.tensor_tensor(dst[:], src[:, :], b, ALU.add).then_inc(sig, 1)

            def product(i, e):
                biased(g, pH3, i, e, 1, s_h3, s_h3b)
                dve.wait_ge(s_silu, i + 1)
                dve.wait_ge(s_h3b, i + 1)
                nc.vector.tensor_tensor(g[:], g[:], h1[:], ALU.mult).then_inc(s_g, 1)

            def result(i, q):
                p = q % 2
                dve.wait_ge(s_y, i + 1)
                dve.wait_ge(s_b2g, i + 1)
                nc.vector.scalar_tensor_tensor(ys[p][:], pY[:, 0:D], gs[q], ys[p][:], ALU.mult, ALU.add).then_inc(s_ys, 1)

            def tile(i, q, first, more):
                p = q % 2
                e = dve.value_load(eid[0:1, bass.ds(i, 1)], min_val=0, max_val=E - 1)
                if more:
                    x_rest(i + 1, 1 - p)
                    gates_of(i + 1, (q + 1) % XBUF)
                pos_wait(dve, s_g, i)
                biased(h1, pH1, i, e, 0, s_h1, s_h1b)
                if not first:
                    g_rest(i - 1)
                product(i, e)
                if not first:
                    result(i - 1, (q - 1) % XBUF)

            dve.wait_ge(s_routed, 1)
            dve.wait_ge(s_bb, 16 * E)
            x_rest(0, 0)
            gates_of(0, 0)
            tile_steps(dve, tile)
            g_rest(NT_SLOTS - 1)
            result(NT_SLOTS - 1, (NT_SLOTS - 1) % XBUF)


def shape_tables():
    f = np.float32
    base = (np.arange(0, D, 2, dtype=f) + f(0.4 * D)) / f(1.4 * D)
    at = np.arange(S, dtype=f)
    scale = np.power(base[None, :], (at[:, None] / f(512.0))).astype(f)
    freqs = (f(1.0) / np.power(f(10000.0), np.arange(D // 2, dtype=f) / f(D // 2))).astype(f)
    angle = (at[:, None] * freqs[None, :]).astype(f)
    sin, cos = np.sin(angle).astype(f), np.cos(angle).astype(f)
    inv = f(1.0) / scale
    tabs = np.stack([cos * scale, sin * scale, cos * inv, sin * inv], 0)
    tabs = np.ascontiguousarray(tabs.transpose(2, 0, 1)).astype(f)
    u, v = np.arange(S, dtype=f)[None, :], np.arange(P, dtype=f)[:, None]
    first = np.where(u >= v, np.power(f(GAMMA), np.maximum(u - v, 0)), 0).astype(f)
    return tabs, first


def routing_constants():
    c = np.zeros((P, C_END), np.float32)
    p = np.arange(P)
    c[:, C_TRI:C_TRI + P] = p[:, None] < p[None, :]
    c[:, C_IOTA:C_IOTA + P] = p[None, :]
    c[:, C_SEG:C_SEG + P] = (p % NJ != 0)[None, :]
    c[:, C_HI:C_HI + KJ] = np.arange(KJ)[None, :]
    c[:, C_TILE:C_TILE + NT_SLOTS] = np.arange(NT_SLOTS)[None, :]
    c[:, C_E:C_E + E] = np.arange(E)[None, :]
    c[:, C_P] = p
    c[:, C_PAD] = TOK + p
    return c


def kernel(**inputs):
    import concourse.bacc as bacc
    from concourse.bass_utils import run_bass_kernel_spmd

    a = {k: np.asarray(v) for k, v in inputs.items()}
    order = np.concatenate([np.arange(0, D, 2), np.arange(1, D, 2)])
    chunks = lambda w: w.reshape(-1, P, w.shape[-1]).transpose(1, 0, 2).reshape(P, -1)

    qkv = np.stack([chunks(a["L0_xattn_Wq"].T[:, order]), chunks(a["L0_xattn_Wk"].T[:, order]),
                    chunks(a["L0_xattn_Wv"].T)], 1)
    f = lambda n: a["L0_ffn_" + n]
    w_all = np.stack([np.stack([chunks(f("W1")[e].T), chunks(f("W3")[e].T), chunks(f("W2")[e].T)]) for e in range(E)])
    w_all = w_all.reshape(E, KINDS, P, 2, UC).transpose(0, 1, 3, 2, 4).reshape(E, UNITS, P, UC)
    lora = np.concatenate([np.concatenate([f("A1")[e], f("B1")[e].T, f("A3")[e], f("B3")[e].T, f("A2")[e], f("B2")[e].T], 1)
                           for e in range(E)])
    tabs, mask = shape_tables()
    arrays = {
        "x": a["x"].reshape(B, TPB, P, D).transpose(0, 2, 1, 3),
        "ctxT": a["ctx_1024"].transpose(0, 2, 1).reshape(B, CH, P, S).transpose(0, 2, 1, 3),
        "wqkv": qkv.reshape(P, 3, CH, D),
        "tables": tabs,
        "mask": mask,
        "gates_in": np.broadcast_to(np.concatenate([a["g_xattn"], a["g_ffn"]])[None, :], (P, 2)),
        "w_all": w_all,
        "lora": lora,
        "biases": np.concatenate([f("b1"), f("b3"), f("b2")], 1),
        "wgT": chunks(f("Wg").T).reshape(P, CH, E),
        "ident": np.eye(P, dtype=np.float32),
        "consts": routing_constants(),
    }
    arrays = {k + "_in": np.ascontiguousarray(v) for k, v in arrays.items()}
    nc = bacc.Bacc("TRN2", target_bir_lowering=False, num_devices=1)
    args = [nc.dram_tensor(k, v.shape, mybir.dt.from_np(v.dtype), kind="ExternalInput").ap() for k, v in arrays.items()]
    out = nc.dram_tensor("out", (B, S, D), F32, kind="ExternalOutput").ap()
    flamingo(nc, *args, out)
    result = run_bass_kernel_spmd(nc, [arrays], core_ids=[0])
    return result.results[0]["out"]
```
